# Optimizing a Trainium2 kernel written in Bass

```python
import numpy as np
import jax
import jax.numpy as jnp

def _softmax(x, axis=-1):
    return jax.nn.softmax(x, axis=axis)

def _gelu(x):
    return jax.nn.gelu(x, approximate=True)

def _silu(x):
    return jax.nn.silu(x)

def _sigmoid(x):
    return jax.nn.sigmoid(x)

def _layernorm(x, axis=-1, eps=1e-05):
    m = jnp.mean(x, axis=axis, keepdims=True)
    v = jnp.var(x, axis=axis, keepdims=True)
    return (x - m) / jnp.sqrt(v + eps)

def _scatter_add(tgt, idx, src, axis=0):
    return tgt.at[idx].add(src)

def _segment_sum(src, seg, n):
    return jax.ops.segment_sum(src, seg, n)
kernel_name = 'mk_pixart_resid_d1_seqx_r8_6e2326'

def setup_inputs(seed: int=0):
    np.random.seed(seed)
    _w = jnp.asarray

    def _rec_inputs():
        import jax
        import jax.numpy as jnp
        _rk = jax.random.key(seed)
        x = -0.0002928 + 1 * jax.random.normal(jax.random.fold_in(_rk, 1), (8, 128, 256), jnp.float32)
        _lenS = 128 - jax.random.randint(jax.random.fold_in(_rk, 7), (8,), 0, max(1, 128 // 4) + 1, jnp.int32)
        _lenS2 = 128 - jax.random.randint(jax.random.fold_in(_rk, 8), (8,), 0, max(1, 128 // 4) + 1, jnp.int32)
        _ctx_2048P = jax.random.normal(jax.random.fold_in(_rk, 11), (8, 16, 256), jnp.float32)
        _ctx_2048c = jax.random.dirichlet(jax.random.fold_in(_rk, 511), 0.3 * jnp.ones((16,), jnp.float32), (8, 128))
        _ctx_2048t = jnp.einsum('bsk,bkd->bsd', _ctx_2048c, _ctx_2048P)
        _ctx_2048t = _ctx_2048t * jax.lax.rsqrt(jnp.mean(jnp.square(_ctx_2048t)) + 1e-12) * 0.953939
        ctx_2048 = -1.39393e-06 + 0.999914 * (_ctx_2048t + 0.3 * jax.random.normal(jax.random.fold_in(_rk, 611), (8, 128, 256), jnp.float32))
        itok_B_779_1933 = jax.random.randint(jax.random.fold_in(_rk, 12), (8,), 779, 1934, jnp.int32)
        return (x, ctx_2048, itok_B_779_1933)
    x, ctx_2048, itok_B_779_1933 = _rec_inputs()

    def _L0_xcond_setup():
        import jax, jax.numpy as jnp
        import numpy as np
        NUM_HEADS = 8
        HEAD_DIM = 64
        AVG_K_LENGTH = 20
        SCALE = 1.0 / (HEAD_DIM ** 0.5 * float(np.log(AVG_K_LENGTH)))
        key = jax.random.key(seed)
        k1, k2, k3, k4 = jax.random.split(key, 4)
        B, HD, LQ, LK = (4, NUM_HEADS * HEAD_DIM, 256, 256)
        q = jax.random.normal(k1, (B, HD, LQ), dtype=jnp.float32)
        k = jax.random.normal(k2, (B, HD, LK), dtype=jnp.float32)
        v = jax.random.normal(k3, (B, HD, LK), dtype=jnp.float32)
        k_length = jax.random.randint(k4, (B,), 64, LK + 1, dtype=jnp.int32)
        return {'q': q, 'k': k, 'v': v, 'k_length': k_length}
    _L0_xcond_all = _L0_xcond_setup()
    _L0_xcond_in = {k: v for k, v in _L0_xcond_all.items() if k in ()}
    del _L0_xcond_all

    def _L0_ffn_setup():
        import jax, jax.numpy as jnp
        import numpy as np
        DIM = 256
        HIDDEN = 1024
        NUM_EXPERTS = 2
        BATCH, SEQ = (4, 128)
        key = jax.random.key(seed)
        k1, k2, k3, k4 = jax.random.split(key, 4)
        x = jax.random.normal(k1, (BATCH, SEQ, DIM), dtype=jnp.float32)
        w_router = jax.random.normal(k2, (NUM_EXPERTS, DIM), dtype=jnp.float32) * (1.0 / np.sqrt(DIM))
        w_fc = jax.random.normal(k3, (NUM_EXPERTS, HIDDEN, DIM), dtype=jnp.float32) * (1.0 / np.sqrt(DIM))
        w_proj = jax.random.normal(k4, (NUM_EXPERTS, DIM, HIDDEN), dtype=jnp.float32) * (1.0 / np.sqrt(HIDDEN))
        return {'x': x, 'w_router': w_router, 'w_fc': w_fc, 'w_proj': w_proj}
    _L0_ffn_all = _L0_ffn_setup()
    _L0_ffn_in = {k: v for k, v in _L0_ffn_all.items() if k in ('w_router', 'w_fc', 'w_proj')}
    del _L0_ffn_all
    return {'x': x, 'ctx_2048': ctx_2048, 'itok_B_779_1933': itok_B_779_1933, 'L0_ffn_w_router': _L0_ffn_in['w_router'], 'L0_ffn_w_fc': _L0_ffn_in['w_fc'], 'L0_ffn_w_proj': _L0_ffn_in['w_proj']}

def reference(x, ctx_2048, itok_B_779_1933, L0_ffn_w_router, L0_ffn_w_fc, L0_ffn_w_proj):
    import jax
    import jax.numpy as jnp

    def _L0_xcond_ref(q, k, v, k_length):
        import jax, jax.numpy as jnp
        import numpy as np
        NUM_HEADS = 8
        HEAD_DIM = 64
        AVG_K_LENGTH = 20
        SCALE = 1.0 / (HEAD_DIM ** 0.5 * float(np.log(AVG_K_LENGTH)))
        b, hd, lq = q.shape
        lk = k.shape[-1]
        d = hd // NUM_HEADS
        qh = q.reshape(b, NUM_HEADS, d, lq)
        kh = k.reshape(b, NUM_HEADS, d, lk)
        vh = v.reshape(b, NUM_HEADS, d, lk)
        s = SCALE * jnp.log(k_length.astype(jnp.float32))[:, None, None, None]
        attn = jnp.einsum('bhdq,bhdk->bhqk', qh, kh)
        attn = jax.nn.softmax(s * attn, axis=-1)
        out = jnp.einsum('bhqk,bhdk->bhdq', attn, vh)
        return out.reshape(b, hd, lq)

    def _L0_ffn_ref(x, w_router, w_fc, w_proj):
        import jax, jax.numpy as jnp
        import numpy as np
        DIM = 256
        HIDDEN = 1024
        NUM_EXPERTS = 2
        BATCH, SEQ = (4, 128)
        bsz, seq, dim = x.shape
        num_experts = w_router.shape[0]
        x_flat = x.reshape(-1, dim)
        logits = x_flat @ w_router.T
        probs = jax.nn.softmax(logits, axis=-1)
        top_idx = jnp.argmax(probs, axis=-1)
        top_weight = jnp.take_along_axis(probs, top_idx[:, None], axis=1)[:, 0]
        h = jnp.einsum('nd,ehd->enh', x_flat, w_fc)
        a = jnp.square(jnp.where(h >= 0, h, 0.5 * h))
        expert_out = jnp.einsum('enh,edh->end', a, w_proj)
        mask = (top_idx[None, :] == jnp.arange(num_experts)[:, None]).astype(x.dtype)
        out = jnp.einsum('end,en->nd', expert_out, mask * top_weight[None, :])
        return out.reshape(bsz, seq, dim)
    x = x + _L0_xcond_ref(_layernorm(x, axis=-1), ctx_2048, ctx_2048, itok_B_779_1933)
    x = x + _L0_ffn_ref(_layernorm(x, axis=-1), L0_ffn_w_router, L0_ffn_w_fc, L0_ffn_w_proj)
    return x

_drawn_inputs = setup_inputs


def setup_inputs(seed=0):
    import zlib

    import numpy as np

    out = dict(_drawn_inputs(seed))
    spreads = {}
    factors = {}
    for name, (base, spread) in spreads.items():
        noise = np.random.default_rng([zlib.crc32(name.encode()), seed]).standard_normal(out[name].shape)
        drawn = base * np.exp(spread * noise) if base else spread * noise
        out[name] = jnp.asarray(drawn.astype(out[name].dtype))
    for name, factor in factors.items():
        out[name] = (out[name] * factor).astype(out[name].dtype)
    return out
```

```python
import concourse.bass as bass
from concourse import mybir
from contextlib import ExitStack
from math import log

B, ROWS, DIM = 8, 128, 256
HEADS, HD = 8, 16
PAIRS = HEADS // 2
KEYS = DIM
HID, EXPERTS = 1024, 2
P = 128
KC = DIM // P
CH = HID // P
CHUNKS = EXPERTS * CH
STEPS = B // 2
SCORE_SCALE = 1.0 / (64 ** 0.5 * log(20))
EPS = 1e-5
MBLK = 96
STACK = MBLK + 2 * HEADS
HEAD_ORDER = [0, 2, 4, 6, 1, 3, 5, 7]
SN_HEADS = [(0,), (1,), (2, 3), (4, 5), (), (6,), (7,), ()]
ST_ORDER = [(0, 1, 2), (3, 4, 5), (6, 7), (), (), (), (), ()]
LAG = 2
NA = 4
WPIECE = 1024
N_WPIECES = CHUNKS * DIM // WPIECE


def build(nc, x, ctx_kv, ctx_t, k_len, w_router, w_fc_t, w_proj_t, consts, out):
    f32, f32r, i32 = mybir.dt.float32, mybir.dt.float32r, mybir.dt.int32
    ALU, ACT, AX = mybir.AluOpType, mybir.ActivationFunctionType, mybir.AxisListType

    with ExitStack() as stack:
        def sb(name, shape, dt=f32):
            return stack.enter_context(nc.sbuf_tensor(name, shape, dt))

        def two(name, shape, dt=f32):
            return [sb(f"{name}{j}", shape, dt) for j in range(2)]

        def bank(name):
            return stack.enter_context(nc.psum_tensor(name, [P, 512], f32))

        def sem(name):
            return stack.enter_context(nc.semaphore(name))

        def sems(name):
            return [sem(f"{name}{j}") for j in range(2)]

        q_scr = [[nc.dram_tensor(f"q_scr{j}{h}", [P, DIM], f32, kind="Internal").ap() for h in "hl"] for j in range(2)]
        k_scr = [[nc.dram_tensor(f"k_scr{j}{h}", [P, DIM], f32, kind="Internal").ap() for h in "hl"] for j in range(2)]

        cst = sb("cst", [P, 200])
        ident = cst[:, 0:128]
        ones_v = [cst[:, 128 + 32 * e:160 + 32 * e] for e in range(2)]
        pick = cst[MBLK:STACK, 192:200]
        len_i = sb("len_i", [P, B], i32)
        len_f = sb("len_f", [P, B])
        len_ln = sb("len_ln", [P, B])
        scale_b = sb("scale_b", [P, B])
        wr = sb("wr", [P, EXPERTS, DIM])
        wr_diff = sb("wr_diff", [P, DIM])
        w_raw = [sb("wfc_raw", [P, CHUNKS * DIM]), sb("wproj_raw", [P, CHUNKS * DIM])]
        w_hi = [sb("wfc_hi", [P, CHUNKS * DIM], f32r), sb("wproj_hi", [P, CHUNKS * DIM], f32r)]
        w_lo = [sb("wfc_lo", [P, CHUNKS * DIM], f32r), sb("wproj_lo", [P, CHUNKS * DIM], f32r)]
        wfc = [w[:, :].rearrange("p (k n) -> p k n", k=KC) for w in (w_hi[0], w_lo[0])]
        wproj = [w[:, :].rearrange("p (c n) -> p c n", c=CHUNKS) for w in (w_hi[1], w_lo[1])]

        x_raw, x_keep, kv_raw = two("x_raw", [P, DIM]), two("x_keep", [P, DIM]), two("kv_raw", [P, DIM])
        v_raw = two("v_raw", [P, KC, ROWS])
        v_pad = two("v_pad", [P, KC * PAIRS, 64])
        xst, xmv, xvar = two("xst", [P, 6]), two("xmv", [P, 2]), two("xvar", [P, 1])
        xln, xrs, xn1, xn2, xsc = (two(n, [P, 1]) for n in ("xln", "xrs", "xn1", "xn2", "xsc"))
        q_f = two("q_f", [P, DIM])
        q_hi, q_lo, k_hi, k_lo = (two(n, [P, DIM], f32r) for n in ("q_hi", "q_lo", "k_hi", "k_lo"))
        q_st = two("q_st", [P, PAIRS, DIM], f32r)
        k_st = two("k_st", [P, 2, PAIRS, KEYS], f32r)
        negm = two("negm", [P, KC, HEADS])
        nm_r = two("nm_r", [P, KC, 2, HEADS], f32r)
        probs = [sb(f"probs{h}", [P, KC, DIM]) for h in range(HEADS)]
        dln, dinv, t1, t2, att = (sb(n, [P, DIM]) for n in ("dln", "dinv", "t1", "t2", "att"))
        x2, x2n = two("x2", [P, DIM]), two("x2n", [P, DIM])
        yst, ymv, yvar = two("yst", [P, 6]), two("ymv", [P, 2]), two("yvar", [P, 1])
        yln, yrs, yn1, yn2, ysc = (two(n, [P, 1]) for n in ("yln", "yrs", "yn1", "yn2", "ysc"))
        dot_out = sb("dot_out", [P, DIM])
        logit = sb("logit", [P, 2])
        nabs, ecoef, e1, wtop = (sb(n, [P, 2]) for n in ("nabs", "ecoef", "e1", "wtop"))
        coef = [sb(f"coef{e}", [P, 2]) for e in range(EXPERTS)]

        xt_hi, xt_lo = sb("xt_hi", [P, KC, 2 * P], f32r), sb("xt_lo", [P, KC, 2 * P], f32r)
        r_buf, l_buf, a_buf = two("r_buf", [P, 2 * P]), two("l_buf", [P, 2 * P]), two("a_buf", [P, 2 * P])
        a_hi, a_lo = ([sb(f"{n}{k}", [P, 2 * P], f32r) for k in range(NA)] for n in ("a_hi", "a_lo"))
        resid = sb("resid", [P, 2, DIM])
        y1, y2 = sb("y1", [P, 2, DIM]), sb("y2", [P, 2, DIM])

        sn = [bank("sn0"), bank("sn1")]
        stp = [bank("st0"), bank("st1")]
        pv = bank("pv")
        misc = bank("misc")
        hps = bank("hps")
        ops_ = bank("ops")

        s_cst, s_len, s_wr = sem("cst_in"), sem("len_in"), sem("router_in")
        s_wraw = sems("w_raw_in")
        s_x, s_kv, s_v, s_keep = sems("x_in"), sems("kv_in"), sems("v_in"), sems("keep_in")
        s_qscr, s_kscr = sems("q_scr_written"), sems("k_scr_written")
        s_qst, s_kst = sems("q_stack_in"), sems("k_stack_in")
        s_out = sem("out_written")
        s_passed = sem("waits_passed")
        s_lenf, s_lenln, s_scale, s_wrd = sem("len_f"), sem("len_ln"), sem("scale_ready"), sem("router_diff")
        s_whi, s_wlo_v, s_wlo_p = sem("w_hi_done"), sem("w_lo_by_vector"), sem("w_lo_by_pool")
        s_zero, s_vzero, s_pick = sems("k_stack_zeroed"), sem("v_pad_zeroed"), sem("pick_rows")
        s_xst, s_xmv, s_xvar, s_xln, s_xrs, s_xn1, s_xn2, s_xsc = (
            sem(n) for n in ("x_stats", "x_moments", "x_var", "x_ln", "x_rstd0", "x_newton1", "x_newton2", "x_scale"))
        s_qf, s_qhi, s_qlo, s_khi, s_klo = (sem(n) for n in ("q_f", "q_hi", "q_lo", "k_hi", "k_lo"))
        s_vpad = sem("v_pad_ready")
        s_sn, s_max, s_nmhi, s_nmlo = sem("scores_qk"), sem("max_done"), sem("negmax_hi"), sem("negmax_lo")
        s_mt, s_mrows = sem("max_transposed"), sem("max_rows")
        s_st, s_exp = sem("scores_kq"), sem("exp_done")
        s_pv = sem("pv_done")
        s_dln, s_dinv, s_t1, s_t2, s_att, s_x2 = (
            sem(n) for n in ("den_ln", "den_inv0", "den_newton1", "den_inv", "attn_out", "x2_ready"))
        s_yst, s_ymv, s_yvar, s_yln, s_yrs, s_yn1, s_yn2, s_ysc = (
            sem(n) for n in ("y_stats", "y_moments", "y_var", "y_ln", "y_rstd0", "y_newton1", "y_newton2", "y_scale"))
        s_x2n, s_logit = sem("x2n_ready"), sem("logit_ready")
        s_nabs, s_ecoef, s_e1, s_wtop, s_c1, s_coef = (
            sem(n) for n in ("neg_abs", "coef_exp", "coef_sum", "top_weight", "coef_1", "coefs_ready"))
        s_xt, s_xthi, s_xtlo = sem("xt_transposed"), sem("xt_hi_ready"), sem("xt_lo_ready")
        s_h, s_r, s_l, s_a, s_ahi, s_alo = (
            sem(n) for n in ("h_ready", "relu_ready", "leaky_ready", "square_ready", "a_hi_ready", "a_lo_ready"))
        s_f2 = sem("a_buffers_free")
        s_o, s_ofree, s_resid, s_y1, s_y2 = (
            sem(n) for n in ("expert_out", "expert_out_free", "resid_ready", "y1_ready", "y2_ready"))

        def wait(eng, s, value):
            if not (isinstance(value, int) and value <= 0):
                eng.wait_ge(s, value)

        def wait_alone(eng, s, value):
            if not (isinstance(value, int) and value <= 0):
                eng.wait_ge(s, value)
                if not isinstance(value, int):
                    eng.sem_inc(s_passed, 1)

        def run_steps(eng, step):
            step(0, ffn=False, last=False)
            with eng.Fori(1, STEPS - 1) as i:
                step(i, ffn=True, last=False)
            step(STEPS - 1, ffn=True, last=True)

        block = stack.enter_context(nc.Block())

        @block.sync
        def _(sp):
            def batch(t, u, j):
                at = t[2 * u + j] if isinstance(u, int) else t[bass.ds(u * 2 + j, 1)].rearrange("o p n -> (o p) n")
                return at

            def load(u, j):
                m = u * 2 + j
                wait_alone(sp, s_qf, m - 1)
                sp.dma_start(x_raw[j][:, :], batch(x, u, j)).then_inc(s_x[j], 16)
                wait_alone(sp, s_khi, m - 1)
                wait_alone(sp, s_klo, m - 1)
                sp.dma_start(kv_raw[j][:, :], batch(ctx_kv, u, j)).then_inc(s_kv[j], 16)

            def load_v(u, j):
                wait_alone(sp, s_vpad, u * 2 + j - 1)
                sp.dma_start(v_raw[j][:, :, :], batch(ctx_t, u, j).rearrange("(c p) n -> p c n", p=P)).then_inc(s_v[j], 16)

            def stack_k(u, j):
                m = u * 2 + j
                wait_alone(sp, s_kst[j], 96 * u)
                wait_alone(sp, s_khi, m + 1)
                sp.dma_start(k_scr[j][0], k_hi[j][:, :].bitcast(f32)).then_inc(s_kscr[j], 16)
                wait_alone(sp, s_klo, m + 1)
                sp.dma_start(k_scr[j][1], k_lo[j][:, :].bitcast(f32)).then_inc(s_kscr[j], 16)

            def stack_q(u, j):
                m = u * 2 + j
                wait_alone(sp, s_qst[j], 48 * u)
                wait_alone(sp, s_qhi, m + 1)
                sp.dma_start(q_scr[j][0], q_hi[j][:, :].bitcast(f32)).then_inc(s_qscr[j], 16)
                wait_alone(sp, s_qlo, m + 1)
                sp.dma_start(q_scr[j][1], q_lo[j][:, :].bitcast(f32)).then_inc(s_qscr[j], 16)

            def read_k(u, j):
                wait_alone(sp, s_st, 8 * (u * 2 + j) - 8)
                wait_alone(sp, s_kscr[j], 32 * u + 32)
                for e in range(2):
                    for blk, part in enumerate((0, 1, 0)):
                        src = k_scr[j][part].rearrange("(g e r) n -> e r g n", g=PAIRS, e=2)[e]
                        row = 32 * blk + HD * e
                        sp.dma_start(k_st[j][row:row + HD, e, :, :].bitcast(f32), src).then_inc(s_kst[j], 16)

            def read_q(u, j):
                wait_alone(sp, s_st, 8 * (u * 2 + j) - 8)
                wait_alone(sp, s_qscr[j], 32 * u + 32)
                for blk, part in enumerate((0, 0, 1)):
                    src = q_scr[j][part].rearrange("(g r) n -> r g n", g=PAIRS)
                    sp.dma_start(q_st[j][32 * blk:32 * blk + 32, :, :].bitcast(f32), src).then_inc(s_qst[j], 16)

            def keep(u, j):
                wait_alone(sp, s_x2, u * 2 + j - 1)
                sp.dma_start(x_keep[j][:, :], batch(x, u, j)).then_inc(s_keep[j], 16)

            def store(g):
                wait_alone(sp, s_y2, g + 1)
                dst = (out[2 * g:2 * g + 2] if isinstance(g, int) else out[bass.ds(g * 2, 2)]).rearrange("t p n -> p t n")
                sp.dma_start(dst, y2[:, :, :]).then_inc(s_out, 16)

            load(0, 0)
            sp.dma_start(cst[:, :], consts).then_inc(s_cst, 16)
            load(0, 1)
            stack_k(0, 0)
            stack_q(0, 0)
            sp.wait_ge(s_zero[0], 1)
            read_k(0, 0)
            read_q(0, 0)
            stack_k(0, 1)
            stack_q(0, 1)
            sp.wait_ge(s_zero[1], 1)
            read_k(0, 1)
            read_q(0, 1)
            load_v(0, 0)
            load_v(0, 1)
            sp.dma_start(w_raw[0][:, :].rearrange("p (k n) -> p k n", k=KC),
                         w_fc_t.rearrange("(k p) n -> p k n", p=P)).then_inc(s_wraw[0], 16)
            sp.dma_start(w_raw[1][:, :].rearrange("p (c n) -> p c n", c=CHUNKS),
                         w_proj_t.rearrange("(c p) n -> p c n", p=P)).then_inc(s_wraw[1], 16)

            def step(i, ffn, last):
                for j in range(2):
                    if not last:
                        load(i + 1, j)
                    keep(i, j)
                    if not last:
                        stack_k(i + 1, j)
                        stack_q(i + 1, j)
                        read_k(i + 1, j)
                        read_q(i + 1, j)
                        load_v(i + 1, j)
                if ffn:
                    store(i - 1)

            run_steps(sp, step)
            store(STEPS - 1)
            sp.wait_ge(s_out, 16 * STEPS)

        @block.gpsimd
        def _(pool):
            pool.memset(k_st[1][:, :, :, :].bitcast(f32), 0.0).then_inc(s_zero[1], 1)
            pool.memset(v_pad[0][:, :, :], 0.0).then_inc(s_vzero, 1)
            pool.memset(v_pad[1][:, :, :], 0.0).then_inc(s_vzero, 1)

            def split_k(u, j):
                m = u * 2 + j
                pool.wait_ge(s_khi, m + 1)
                wait(pool, s_kscr[j], 32 * u)
                pool.tensor_tensor(k_lo[j][:, :], kv_raw[j][:, :], k_hi[j][:, :].bitcast(f32), ALU.subtract).then_inc(s_klo, 1)

            def pad_v(u, j):
                m = u * 2 + j
                pool.wait_ge(s_v[j], 16 * u + 16)
                wait_alone(pool, s_pv, 2 * m - 2)
                src = v_raw[j][:, :, :].rearrange("p c (g n) -> p (c g) n", g=PAIRS)
                pool.tensor_copy(v_pad[j][:, :, 0:16], src[:, :, 0:16])
                pool.tensor_copy(v_pad[j][:, :, 48:64], src[:, :, 16:32]).then_inc(s_vpad, 1)

            def split_w(w, n):
                at = slice(n * WPIECE, (n + 1) * WPIECE)
                pool.wait_ge(s_whi, w * N_WPIECES + n + 1)
                pool.tensor_tensor(w_lo[w][:, at], w_raw[w][:, at], w_hi[w][:, at].bitcast(f32), ALU.subtract).then_inc(s_wlo_p, 1)

            def square(g, c):
                pool.wait_ge(s_l, g * 16 + (c + 1))
                pool.tensor_tensor(a_buf[c % 2][:, :], l_buf[c % 2][:, :], l_buf[c % 2][:, :], ALU.mult).then_inc(s_a, 1)

            split_k(0, 0)
            split_k(0, 1)
            pool.wait_ge(s_vzero, 2)
            pad_v(0, 0)
            pad_v(0, 1)

            def step(i, ffn, last):
                for j in range(2):
                    for s in range(CH):
                        if ffn:
                            square(i - 1, CH * j + s)
                        elif s >= 4:
                            split_w(j, s - 4)
                        if s == 1 and not last:
                            split_k(i + 1, j)
                        if s == 6 and not last:
                            pad_v(i + 1, j)

            run_steps(pool, step)
            for c in range(CHUNKS):
                square(STEPS - 1, c)

        @block.scalar
        def _(act):
            def k_part_hi(u, j):
                m = u * 2 + j
                act.wait_ge(s_kv[j], 16 * u + 16)
                wait(act, s_kscr[j], 32 * u)
                act.activation(k_hi[j][:, :], kv_raw[j][:, :], ACT.Copy).then_inc(s_khi, 1)

            def q_part_hi(u, j):
                m = u * 2 + j
                act.wait_ge(s_qf, m + 1)
                wait(act, s_qscr[j], 32 * u)
                act.activation(q_hi[j][:, :], q_f[j][:, :], ACT.Copy).then_inc(s_qhi, 1)

            def rstd(m, s_in, var, ln, rs, s_mid, s_done):
                act.wait_ge(s_in, m + 1)
                act.activation(ln[:, :], var[:, :], ACT.Ln).then_inc(s_mid, 1)
                act.wait_ge(s_mid, m + 1)
                act.activation(rs[:, :], ln[:, :], ACT.Exp, scale=-0.5).then_inc(s_done, 1)

            def x_rstd(u, j):
                rstd(u * 2 + j, s_xvar, xvar[j], xln[j], xrs[j], s_xln, s_xrs)

            def y_rstd(u, j):
                rstd(u * 2 + j, s_yvar, yvar[j], yln[j], yrs[j], s_yln, s_yrs)

            def max_rows(i, j):
                b = i * 2 + j
                act.wait_ge(s_mt, b + 1)
                act.wait_ge(s_qst[j], 48 * i + 48)
                act.activation(q_st[j][MBLK:STACK, :, :],
                               misc[0:2 * HEADS, 0:DIM].unsqueeze(1).to_broadcast([2 * HEADS, PAIRS, DIM]),
                               ACT.Copy).then_inc(s_mrows, 1)

            def exp(i, j, k):
                b = i * 2 + j
                act.wait_ge(s_st, 8 * b + (k + 1))
                wait(act, s_pv, b * 2 - 1 if k < 4 else b * 2)
                act.activation(probs[HEAD_ORDER[k]][:, :, :], stp[k % 2][:, :].rearrange("p (c n) -> p c n", c=KC),
                               ACT.Exp).then_inc(s_exp, 1)

            def den_inverse(i, j):
                b = i * 2 + j
                act.wait_ge(s_pv, b * 2 + 2)
                wait(act, s_t2, b)
                act.activation(dln[:, :], pv[:, DIM:2 * DIM], ACT.Ln).then_inc(s_dln, 1)
                act.wait_ge(s_dln, b + 1)
                act.activation(dinv[:, :], dln[:, :], ACT.Exp, scale=-1.0).then_inc(s_dinv, 1)

            def relu(g, c):
                act.wait_ge(s_h, g * 16 + (c + 1))
                act.activation(r_buf[c % 2][:, :], hps[:, 0:2 * P], ACT.Relu, scale=0.5).then_inc(s_r, 1)

            def square_hi(g, c):
                act.wait_ge(s_l, g * 16 + (c + 1))
                act.wait_ge(s_f2, g * 16 + (c + 1))
                act.activation(a_hi[c % NA][:, :], l_buf[c % 2][:, :], ACT.Square).then_inc(s_ahi, 1)

            def coef_exp(g):
                act.wait_ge(s_nabs, g + 1)
                act.activation(ecoef[:, :], nabs[:, :], ACT.Exp).then_inc(s_ecoef, 1)

            def xt_part_hi(i):
                act.wait_ge(s_xt, i + 1)
                act.activation(xt_hi[:, :, :], misc[:, :].rearrange("p (c n) -> p c n", c=KC), ACT.Copy).then_inc(s_xthi, 1)

            def split_w(w, n):
                at = slice(n * WPIECE, (n + 1) * WPIECE)
                act.wait_ge(s_wraw[w], 16)
                act.activation(w_hi[w][:, at], w_raw[w][:, at], ACT.Copy).then_inc(s_whi, 1)

            def pick_rows(j):
                act.activation(k_st[j][MBLK:STACK, :, :, :].rearrange("p e g n -> p (e g) n"),
                               pick.unsqueeze(2).to_broadcast([2 * HEADS, HEADS, KEYS]), ACT.Copy).then_inc(s_pick, 1)

            act.preload_act_table_set("natural_log_exp_and_others")
            act.dma_start(len_i[:, :], k_len.partition_broadcast(P)).then_inc(s_len, 16)
            act.dma_start(wr[:, :, :], w_router.partition_broadcast(P)).then_inc(s_wr, 16)
            k_part_hi(0, 0)
            act.wait_ge(s_lenf, 1)
            act.activation(len_ln[:, :], len_f[:, :], ACT.Ln).then_inc(s_lenln, 1)
            x_rstd(0, 0)
            q_part_hi(0, 0)
            k_part_hi(0, 1)
            x_rstd(0, 1)
            q_part_hi(0, 1)
            act.wait_ge(s_cst, 16)
            for j in range(2):
                act.wait_ge(s_zero[j], 1)
                pick_rows(j)

            max_rows(0, 0)

            def step(i, ffn, last):
                for j in range(2):
                    ni, nj, ahead = i + j, 1 - j, not (last and j == 1)
                    for s in range(CH):
                        c = CH * j + s
                        if ffn:
                            relu(i - 1, c)
                        if s == 4:
                            den_inverse(i, j)
                        for k in ST_ORDER[s][:2]:
                            exp(i, j, k)
                        if s == 5:
                            y_rstd(i, j)
                        if ffn:
                            square_hi(i - 1, c)
                        for k in ST_ORDER[s][2:]:
                            exp(i, j, k)
                        if s == 0 and j == 0 and ffn:
                            coef_exp(i - 1)
                        if s == 0 and not last:
                            k_part_hi(i + 1, j)
                            x_rstd(i + 1, j)
                        if s == 1 and not last:
                            q_part_hi(i + 1, j)
                        if not ffn and s >= 4:
                            split_w(j, s - 4)
                        if s == 7 and ahead:
                            max_rows(ni, nj)
                xt_part_hi(i)

            run_steps(act, step)
            g = STEPS - 1
            for c in range(CHUNKS):
                relu(g, c)
                square_hi(g, c)
                if c == 0:
                    coef_exp(g)

        @block.vector
        def _(dve):
            def moments(m, src, st, mv, var, s_st_, s_mv_, s_var_):
                dve.bn_stats(st[:, :], src).then_inc(s_st_, 1)
                wait_alone(dve, s_st_, m + 1)
                dve.bn_aggr(mv[:, :], st[:, :]).then_inc(s_mv_, 1)
                dve.wait_ge(s_mv_, m + 1)
                dve.tensor_scalar(var[:, :], mv[:, 1:2], EPS, None, ALU.add).then_inc(s_var_, 1)

            def newton(m, var, rs, n1, n2, sc, extra, s_rs_, s_n1_, s_n2_, s_sc_):
                dve.wait_ge(s_rs_, m + 1)
                dve.scalar_tensor_tensor(n1[:, :], rs[:, :], rs[:, 0:1], var[:, :], ALU.mult, ALU.mult).then_inc(s_n1_, 1)
                dve.wait_ge(s_n1_, m + 1)
                dve.tensor_scalar(n2[:, :], n1[:, :], -0.5, 1.5, ALU.mult, ALU.add).then_inc(s_n2_, 1)
                dve.wait_ge(s_n2_, m + 1)
                dve.scalar_tensor_tensor(sc[:, :], n2[:, :], extra, rs[:, :], ALU.mult, ALU.mult).then_inc(s_sc_, 1)

            def x_moments(u, j):
                dve.wait_ge(s_x[j], 16 * u + 16)
                moments(u * 2 + j, x_raw[j][:, :], xst[j], xmv[j], xvar[j], s_xst, s_xmv, s_xvar)

            def q_normalise(u, j):
                m = u * 2 + j
                sc_b = scale_b[:, m:m + 1] if isinstance(u, int) else scale_b[:, bass.ds(m, 1)]
                newton(m, xvar[j], xrs[j], xn1[j], xn2[j], xsc[j], sc_b, s_xrs, s_xn1, s_xn2, s_xsc)
                dve.wait_ge(s_xsc, m + 1)
                dve.tensor_scalar(q_f[j][:, :], x_raw[j][:, :], xmv[j][:, 0:1], xsc[j][:, 0:1],
                                  ALU.subtract, ALU.mult).then_inc(s_qf, 1)

            def q_part_lo(u, j):
                m = u * 2 + j
                dve.wait_ge(s_qhi, m + 1)
                wait(dve, s_qscr[j], 32 * u)
                dve.tensor_tensor(q_lo[j][:, :], q_f[j][:, :], q_hi[j][:, :].bitcast(f32), ALU.subtract).then_inc(s_qlo, 1)

            def row_max(n, j, h):
                dve.wait_ge(s_sn, 8 * n + (h + 1))
                dve.tensor_reduce(negm[j][:, :, h], sn[h % 2][:, :].rearrange("p (c n) -> p c n", c=KC),
                                  AX.X, ALU.max, negate=True).then_inc(s_max, 1)

            def split_max(n, j):
                dve.wait_ge(s_max, 8 * n + 8)
                dve.tensor_copy(nm_r[j][:, :, 0, :], negm[j][:, :, :]).then_inc(s_nmhi, 1)
                dve.wait_ge(s_nmhi, n + 1)
                dve.tensor_tensor(nm_r[j][:, :, 1, :], negm[j][:, :, :], nm_r[j][:, :, 0, :].bitcast(f32),
                                  ALU.subtract).then_inc(s_nmlo, 1)

            def attention_out(i, j):
                b = i * 2 + j
                dve.wait_ge(s_dinv, b + 1)
                dve.tensor_tensor(t1[:, :], pv[:, DIM:2 * DIM], dinv[:, :], ALU.mult).then_inc(s_t1, 1)
                dve.wait_ge(s_t1, b + 1)
                dve.scalar_tensor_tensor(t2[:, :], t1[:, :], -2.0, dinv[:, :], ALU.add, ALU.mult).then_inc(s_t2, 1)
                dve.wait_ge(s_t2, b + 1)
                dve.tensor_tensor(att[:, :], pv[:, 0:DIM], t2[:, :], ALU.mult).then_inc(s_att, 1)
                dve.wait_ge(s_att, b + 1)
                dve.wait_ge(s_keep[j], 16 * i + 16)
                dve.tensor_tensor(x2[j][:, :], x_keep[j][:, :], att[:, :], ALU.subtract).then_inc(s_x2, 1)

            def x2_moments(i, j):
                b = i * 2 + j
                dve.wait_ge(s_x2, b + 1)
                moments(b, x2[j][:, :], yst[j], ymv[j], yvar[j], s_yst, s_ymv, s_yvar)

            def x2_normalise(i, j):
                b = i * 2 + j
                newton(b, yvar[j], yrs[j], yn1[j], yn2[j], ysc[j], 1.0, s_yrs, s_yn1, s_yn2, s_ysc)
                dve.wait_ge(s_ysc, b + 1)
                dve.tensor_scalar(x2n[j][:, :], x2[j][:, :], ymv[j][:, 0:1], ysc[j][:, 0:1],
                                  ALU.subtract, ALU.mult).then_inc(s_x2n, 1)
                dve.wait_ge(s_x2n, b + 1)
                dve.scalar_tensor_tensor(dot_out[:, :], x2n[j][:, :], 1.0, wr_diff[:, :], ALU.mult, ALU.mult,
                                         accum_out=logit[:, j:j + 1]).then_inc(s_logit, 1)

            def coef_start(g):
                dve.wait_ge(s_logit, g * 2 + 2)
                dve.tensor_scalar(e1[:, :], logit[:, :], -1.0, None, ALU.mult).then_inc(s_e1, 1)
                dve.wait_ge(s_e1, g * 2 + 1)
                dve.tensor_tensor(nabs[:, :], logit[:, :], e1[:, :], ALU.min).then_inc(s_nabs, 1)

            def coef_end(g):
                dve.wait_ge(s_ecoef, g + 1)
                dve.tensor_scalar(e1[:, :], ecoef[:, :], 1.0, None, ALU.add).then_inc(s_e1, 1)
                dve.wait_ge(s_e1, g * 2 + 2)
                dve.reciprocal(wtop[:, :], e1[:, :]).then_inc(s_wtop, 1)
                dve.wait_ge(s_wtop, g + 1)
                dve.scalar_tensor_tensor(coef[1][:, :], logit[:, :], 0.0, wtop[:, :], ALU.is_gt, ALU.mult).then_inc(s_c1, 1)
                dve.scalar_tensor_tensor(coef[0][:, :], logit[:, :], 0.0, wtop[:, :], ALU.is_le, ALU.mult).then_inc(s_coef, 1)

            def residual_copy(g):
                dve.wait_ge(s_x2, g * 2 + 2)
                for t in range(2):
                    last = dve.tensor_copy(resid[:, t, :], x2[t][:, :])
                last.then_inc(s_resid, 1)

            def leaky(g, c):
                dve.wait_ge(s_r, g * 16 + (c + 1))
                dve.scalar_tensor_tensor(l_buf[c % 2][:, :], hps[:, 0:2 * P], 0.5, r_buf[c % 2][:, :],
                                         ALU.mult, ALU.add).then_inc(s_l, 1)

            def square_lo(g, c):
                dve.wait_ge(s_a, g * 16 + (c + 1))
                dve.wait_ge(s_ahi, g * 16 + (c + 1))
                dve.tensor_tensor(a_lo[c % NA][:, :], a_buf[c % 2][:, :], a_hi[c % NA][:, :].bitcast(f32),
                                  ALU.subtract).then_inc(s_alo, 1)

            def expert_out(g, e):
                dve.wait_ge(s_o, g * 2 + (e + 1))
                if e == 0:
                    dve.wait_ge(s_coef, g + 1)
                    dve.wait_ge(s_resid, g + 1)
                    for t in range(2):
                        last = dve.scalar_tensor_tensor(y1[:, t, :], ops_[:, t * DIM:(t + 1) * DIM], coef[0][:, t:t + 1],
                                                        resid[:, t, :], ALU.mult, ALU.add)
                    last.then_inc(s_ofree, 1)
                else:
                    dve.wait_ge(s_c1, g + 1)
                    dve.wait_ge(s_ofree, g * 2 + 1)
                    wait(dve, s_out, 16 * g)
                    for t in range(2):
                        last = dve.scalar_tensor_tensor(y2[:, t, :], ops_[:, t * DIM:(t + 1) * DIM], coef[1][:, t:t + 1],
                                                        y1[:, t, :], ALU.mult, ALU.add)
                    last.then_inc(s_ofree, 1)
                    dve.wait_ge(s_ofree, g * 2 + 2)
                    dve.sem_inc(s_y2, 1)

            def xt_part_lo(i):
                dve.wait_ge(s_xthi, i + 1)
                dve.tensor_tensor(xt_lo[:, :, :], misc[:, :].rearrange("p (c n) -> p c n", c=KC),
                                  xt_hi[:, :, :].bitcast(f32), ALU.subtract).then_inc(s_xtlo, 1)

            dve.memset(k_st[0][:, :, :, :].bitcast(f32), 0.0).then_inc(s_zero[0], 1)
            x_moments(0, 0)
            dve.wait_ge(s_len, 16)
            dve.tensor_copy(len_f[:, :], len_i[:, :]).then_inc(s_lenf, 1)
            dve.wait_ge(s_lenln, 1)
            dve.tensor_scalar(scale_b[:, :], len_ln[:, :], SCORE_SCALE, None, ALU.mult).then_inc(s_scale, 1)
            dve.wait_ge(s_scale, 1)
            q_normalise(0, 0)
            x_moments(0, 1)
            q_part_lo(0, 0)
            q_normalise(0, 1)
            q_part_lo(0, 1)
            dve.wait_ge(s_wr, 16)
            dve.tensor_tensor(wr_diff[:, :], wr[:, 1, :], wr[:, 0, :], ALU.subtract).then_inc(s_wrd, 1)
            dve.wait_ge(s_wrd, 1)
            for h in range(HEADS):
                row_max(0, 0, h)
            split_max(0, 0)

            def step(i, ffn, last):
                for j in range(2):
                    n, jn, ahead = i * 2 + (j + 1), 1 - j, not (last and j == 1)
                    for s in range(CH):
                        c = CH * j + s
                        if ffn:
                            leaky(i - 1, c)
                        for h in SN_HEADS[s][:1] if ahead else ():
                            row_max(n, jn, h)
                        if s == 0 and ffn and j == 0:
                            coef_start(i - 1)
                            residual_copy(i - 1)
                        if s == LAG - 1 and ffn and j == 0:
                            coef_end(i - 1)
                        if s == LAG - 1 and ffn and j == 1:
                            expert_out(i - 1, 0)
                        if s == 0 and not last:
                            x_moments(i + 1, j)
                        if s == 1 and not last:
                            q_normalise(i + 1, j)
                        if s == 5:
                            x2_moments(i, j)
                        if ffn and c > 0:
                            square_lo(i - 1, c - 1)
                        if s == 2 and not last:
                            q_part_lo(i + 1, j)
                        if s == 4:
                            attention_out(i, j)
                        if s == 6:
                            x2_normalise(i, j)
                        for h in SN_HEADS[s][1:] if ahead else ():
                            row_max(n, jn, h)
                        if s == 6 and ahead:
                            split_max(n, jn)
                if ffn:
                    square_lo(i - 1, CHUNKS - 1)
                xt_part_lo(i)
                if ffn:
                    expert_out(i - 1, 1)

            run_steps(dve, step)
            g = STEPS - 1
            for c in range(CHUNKS):
                leaky(g, c)
                if c == 0:
                    coef_start(g)
                    residual_copy(g)
                if c == LAG - 1:
                    coef_end(g)
                if c > 0:
                    square_lo(g, c - 1)
                if c == CH + LAG - 1:
                    expert_out(g, 0)
            square_lo(g, CHUNKS - 1)
            expert_out(g, 1)

        @block.tensor
        def _(pe):
            def scores_qk(i, j, h):
                b = i * 2 + j
                if h == 0:
                    pe.wait_ge(s_qst[j], 48 * i + 48)
                    pe.wait_ge(s_kst[j], 96 * i + 96)
                wait(pe, s_max, 8 * b + (h - 1))
                for qc in range(KC):
                    last = pe.matmul(sn[h % 2][:, qc * KEYS:(qc + 1) * KEYS],
                                     q_st[j][0:MBLK, h // 2, qc * P:(qc + 1) * P], k_st[j][0:MBLK, h % 2, h // 2, :],
                                     start=(qc == 0), stop=True, skip_group_check=True)
                last.then_inc(s_sn, 1)

            def max_transpose(i, j):
                b = i * 2 + j
                pe.wait_ge(s_nmlo, b + 1)
                wait(pe, s_mrows, b)
                wait(pe, s_xtlo, i - (1 - j))
                for qc in range(KC):
                    last = pe.transpose(misc[0:2 * HEADS, qc * P:(qc + 1) * P],
                                        nm_r[j][:, qc, :, :].rearrange("p a h -> p (a h)").bitcast(f32), ident)
                last.then_inc(s_mt, 1)

            def scores_kq(i, j, k):
                b, h = i * 2 + j, HEAD_ORDER[k]
                if k == 0:
                    pe.wait_ge(s_mrows, b + 1)
                wait(pe, s_exp, 8 * b + (k - 1))
                for kc in range(KC):
                    last = pe.matmul(stp[k % 2][:, kc * DIM:(kc + 1) * DIM],
                                     k_st[j][0:STACK, h % 2, h // 2, kc * P:(kc + 1) * P], q_st[j][0:STACK, h // 2, :],
                                     start=(kc == 0), stop=True, skip_group_check=True)
                last.then_inc(s_st, 1)

            def values(i, j, e):
                b = i * 2 + j
                pe.wait_ge(s_exp, 8 * b + 4 + 4 * e)
                if e == 0:
                    pe.wait_ge(s_vpad, b + 1)
                    wait(pe, s_att, b)
                for kc in range(KC):
                    for den in range(2):
                        for g in range(PAIRS):
                            lhs = ones_v[e] if den else v_pad[j][:, kc * PAIRS + g, 32 * e:32 * e + 32]
                            last = pe.matmul(pv[32 * g:32 * g + 32, den * DIM:(den + 1) * DIM], lhs,
                                             probs[2 * g + e][:, kc, :],
                                             start=(e == 0 and kc == 0 and den == 0), stop=(e == 1 and kc == 1),
                                             skip_group_check=True)
                last.then_inc(s_pv, 1)

            def ffn1(g, c):
                wait(pe, s_l, g * 16 + c)
                if c == 0:
                    pe.wait_ge(s_xthi, g + 1)
                    pe.wait_ge(s_xtlo, g + 1)
                for kc in range(KC):
                    for w, xt in ((0, xt_hi), (1, xt_hi), (0, xt_lo)):
                        last = pe.matmul(hps[:, 0:2 * P], wfc[w][:, kc, c * P:(c + 1) * P], xt[:, kc, :],
                                         start=(kc == 0 and w == 0 and xt is xt_hi), stop=(kc == KC - 1 and xt is xt_lo))
                last.then_inc(s_h, 1)

            def ffn2(g, c):
                pe.wait_ge(s_ahi, g * 16 + (c + 1))
                if c % CH == 0:
                    wait(pe, s_ofree, g * 2 + c // CH)
                for part in range(3):
                    if part == 2:
                        pe.wait_ge(s_alo, g * 16 + (c + 1))
                    for t in range(2):
                        a, w = ((a_hi, 0), (a_hi, 1), (a_lo, 0))[part]
                        last = pe.matmul(ops_[:, t * DIM:(t + 1) * DIM], a[c % NA][:, t * P:(t + 1) * P], wproj[w][:, c, :],
                                         start=(c % CH == 0 and part == 0 and t == 0), stop=(c % CH == CH - 1 and part == 2),
                                         skip_group_check=True)
                last.then_inc(s_f2, 1)
                if c % CH == CH - 1:
                    pe.wait_ge(s_f2, g * 16 + (c + 1 + NA))
                    pe.sem_inc(s_o, 1)

            def x_transpose(i, last):
                pe.wait_ge(s_x2n, i * 2 + 2)
                pe.wait_ge(s_mrows, i * 2 + (2 if last else 3))
                for t in range(2):
                    for kc in range(KC):
                        last = pe.transpose(misc[:, kc * 2 * P + t * P:kc * 2 * P + (t + 1) * P],
                                            x2n[t][:, kc * P:(kc + 1) * P], ident)
                last.then_inc(s_xt, 1)

            pe.sem_inc(s_f2, NA)
            pe.wait_ge(s_cst, 16)
            for h in range(HEADS):
                scores_qk(0, 0, h)
            max_transpose(0, 0)
            pe.wait_ge(s_pick, 2)

            def step(i, ffn, last):
                for j in range(2):
                    ni, nj, ahead = i + j, 1 - j, not (last and j == 1)
                    for s in range(CH):
                        c = CH * j + s
                        if ffn:
                            ffn1(i - 1, c)
                        for k in ST_ORDER[s]:
                            scores_kq(i, j, k)
                        if s == 2:
                            values(i, j, 0)
                        if s == 3:
                            values(i, j, 1)
                        for h in SN_HEADS[s] if ahead else ():
                            scores_qk(ni, nj, h)
                        if s == 7 and ahead:
                            max_transpose(ni, nj)
                        if ffn and c >= LAG:
                            ffn2(i - 1, c - LAG)
                x_transpose(i, last)
                if ffn:
                    for c in range(CHUNKS - LAG, CHUNKS):
                        ffn2(i - 1, c)
                else:
                    pe.wait_ge(s_wlo_p, 2 * N_WPIECES)

            run_steps(pe, step)
            g = STEPS - 1
            for c in range(CHUNKS + LAG):
                if c < CHUNKS:
                    ffn1(g, c)
                if c >= LAG:
                    ffn2(g, c - LAG)


def kernel(**inputs):
    import numpy as np
    import concourse.bacc as bacc
    from concourse.bass_utils import run_bass_kernel_spmd

    ctx = inputs["ctx_2048"]
    consts = np.zeros((P, 200), np.float32)
    consts[:, 0:128] = np.eye(128, dtype=np.float32)
    for e in range(2):
        consts[:, 128 + 32 * e + HD * e:128 + 32 * e + HD * e + HD] = 1.0
    for part in range(2):
        for h in range(HEADS):
            consts[MBLK + HEADS * part + h, 192 + PAIRS * (h % 2) + h // 2] = 1.0
    arrays = {
        "x": np.ascontiguousarray(inputs["x"]),
        "ctx_kv": np.ascontiguousarray(ctx),
        "ctx_t": np.ascontiguousarray(np.transpose(ctx, (0, 2, 1))),
        "k_len": np.ascontiguousarray(inputs["itok_B_779_1933"]),
        "w_router": np.ascontiguousarray(inputs["L0_ffn_w_router"]),
        "w_fc_t": np.ascontiguousarray(np.transpose(inputs["L0_ffn_w_fc"], (2, 0, 1)).reshape(DIM, EXPERTS * HID)),
        "w_proj_t": np.ascontiguousarray(np.transpose(inputs["L0_ffn_w_proj"], (0, 2, 1)).reshape(EXPERTS * HID, DIM)),
        "consts": consts,
    }
    nc = bacc.Bacc("TRN2", target_bir_lowering=False, num_devices=1)
    aps = {n: nc.dram_tensor(n, a.shape, mybir.dt.from_np(a.dtype), kind="ExternalInput").ap() for n, a in arrays.items()}
    out = nc.dram_tensor("out", (B, ROWS, DIM), mybir.dt.float32, kind="ExternalOutput").ap()
    build(nc, aps["x"], aps["ctx_kv"], aps["ctx_t"], aps["k_len"], aps["w_router"], aps["w_fc_t"], aps["w_proj_t"],
          aps["consts"], out)
    r = run_bass_kernel_spmd(nc, [arrays], core_ids=[0])
    return r.results[0]["out"]
```

```python
import concourse.bass as bass
from concourse import mybir
from contextlib import ExitStack
from math import log

B, ROWS, DIM = 8, 128, 256
HEADS, HD = 8, 16
PAIRS = HEADS // 2
KEYS = DIM
HID, EXPERTS = 1024, 2
P = 128
KC = DIM // P
CH = HID // P
CHUNKS = EXPERTS * CH
STEPS = B // 2
SCORE_SCALE = 1.0 / (64 ** 0.5 * log(20))
EPS = 1e-5
MBLK = 96
STACK = MBLK + 2 * HEADS
HEAD_ORDER = [0, 2, 4, 6, 1, 3, 5, 7]
LAG = 2
NA = 4
WPIECE = 1024
N_WPIECES = CHUNKS * DIM // WPIECE


def build(nc, x, ctx_kv, ctx_t, k_len, w_router, w_fc_t, w_proj_t, consts, out):
    f32, f32r, i32 = mybir.dt.float32, mybir.dt.float32r, mybir.dt.int32
    ALU, ACT, AX = mybir.AluOpType, mybir.ActivationFunctionType, mybir.AxisListType

    with ExitStack() as stack:
        def sb(name, shape, dt=f32):
            return stack.enter_context(nc.sbuf_tensor(name, shape, dt))

        def two(name, shape, dt=f32):
            return [sb(f"{name}{j}", shape, dt) for j in range(2)]

        def bank(name):
            return stack.enter_context(nc.psum_tensor(name, [P, 512], f32))

        def sem(name):
            return stack.enter_context(nc.semaphore(name))

        def sems(name):
            return [sem(f"{name}{j}") for j in range(2)]

        q_scr = [[nc.dram_tensor(f"q_scr{j}{h}", [P, DIM], f32, kind="Internal").ap() for h in "hl"] for j in range(2)]
        k_scr = [[nc.dram_tensor(f"k_scr{j}{h}", [P, DIM], f32, kind="Internal").ap() for h in "hl"] for j in range(2)]

        cst = sb("cst", [P, 200])
        ident = cst[:, 0:128]
        ones_v = [cst[:, 128 + 32 * e:160 + 32 * e] for e in range(2)]
        pick = cst[MBLK:STACK, 192:200]
        len_i = sb("len_i", [P, B], i32)
        len_f = sb("len_f", [P, B])
        len_ln = sb("len_ln", [P, B])
        scale_b = sb("scale_b", [P, B])
        wr = sb("wr", [P, EXPERTS, DIM])
        wr_diff = sb("wr_diff", [P, DIM])
        w_raw = [sb("wfc_raw", [P, CHUNKS * DIM]), sb("wproj_raw", [P, CHUNKS * DIM])]
        w_hi = [sb("wfc_hi", [P, CHUNKS * DIM], f32r), sb("wproj_hi", [P, CHUNKS * DIM], f32r)]
        w_lo = [sb("wfc_lo", [P, CHUNKS * DIM], f32r), sb("wproj_lo", [P, CHUNKS * DIM], f32r)]
        wfc = [w[:, :].rearrange("p (k n) -> p k n", k=KC) for w in (w_hi[0], w_lo[0])]
        wproj = [w[:, :].rearrange("p (c n) -> p c n", c=CHUNKS) for w in (w_hi[1], w_lo[1])]

        x_raw, x_keep, kv_raw = two("x_raw", [P, DIM]), two("x_keep", [P, DIM]), two("kv_raw", [P, DIM])
        v_raw = two("v_raw", [P, KC, ROWS])
        v_pad = two("v_pad", [P, KC * PAIRS, 64])
        xst, xmv, xvar = two("xst", [P, 6]), two("xmv", [P, 2]), two("xvar", [P, 1])
        xln, xrs, xn1, xn2, xsc = (two(n, [P, 1]) for n in ("xln", "xrs", "xn1", "xn2", "xsc"))
        q_f = two("q_f", [P, DIM])
        q_hi, q_lo, k_hi, k_lo = (two(n, [P, DIM], f32r) for n in ("q_hi", "q_lo", "k_hi", "k_lo"))
        q_st = two("q_st", [P, PAIRS, DIM], f32r)
        k_st = two("k_st", [P, 2, PAIRS, KEYS], f32r)
        negm = two("negm", [P, KC, HEADS])
        nm_r = two("nm_r", [P, KC, 2, HEADS], f32r)
        probs = [sb(f"probs{h}", [P, KC, DIM]) for h in range(HEADS)]
        dln, dinv, t1, t2, att = (sb(n, [P, DIM]) for n in ("dln", "dinv", "t1", "t2", "att"))
        x2, x2n = two("x2", [P, DIM]), two("x2n", [P, DIM])
        yst, ymv, yvar = two("yst", [P, 6]), two("ymv", [P, 2]), two("yvar", [P, 1])
        yln, yrs, yn1, yn2, ysc = (two(n, [P, 1]) for n in ("yln", "yrs", "yn1", "yn2", "ysc"))
        dot_out = sb("dot_out", [P, DIM])
        logit = sb("logit", [P, 2])
        nabs, ecoef, e1, wtop = (sb(n, [P, 2]) for n in ("nabs", "ecoef", "e1", "wtop"))
        coef = [sb(f"coef{e}", [P, 2]) for e in range(EXPERTS)]

        xt_hi, xt_lo = sb("xt_hi", [P, KC, 2 * P], f32r), sb("xt_lo", [P, KC, 2 * P], f32r)
        r_buf, l_buf, a_buf = two("r_buf", [P, 2 * P]), two("l_buf", [P, 2 * P]), two("a_buf", [P, 2 * P])
        a_hi, a_lo = ([sb(f"{n}{k}", [P, 2 * P], f32r) for k in range(NA)] for n in ("a_hi", "a_lo"))
        resid = sb("resid", [P, 2, DIM])
        y1, y2 = sb("y1", [P, 2, DIM]), sb("y2", [P, 2, DIM])

        sn = bank("sn")
        stp = [bank("st0"), bank("st1")]
        pv = bank("pv")
        misc = bank("misc")
        hps = [bank("h0"), bank("h1")]
        ops_ = bank("ops")
        sn_first = [sn, ops_]

        s_cst, s_len, s_wr = sem("cst_in"), sem("len_in"), sem("router_in")
        s_wraw = sems("w_raw_in")
        s_x, s_kv, s_v, s_keep = sems("x_in"), sems("kv_in"), sems("v_in"), sems("keep_in")
        s_qscr, s_kscr = sems("q_scr_written"), sems("k_scr_written")
        s_qst, s_kst = sems("q_stack_in"), sems("k_stack_in")
        s_out = sem("out_written")
        s_passed = sem("waits_passed")
        s_lenf, s_lenln, s_scale, s_wrd = sem("len_f"), sem("len_ln"), sem("scale_ready"), sem("router_diff")
        s_whi, s_wlo_v, s_wlo_p = sem("w_hi_done"), sem("w_lo_by_vector"), sem("w_lo_by_pool")
        s_zero, s_vzero, s_pick = sems("k_stack_zeroed"), sem("v_pad_zeroed"), sem("pick_rows")
        s_xst, s_xmv, s_xvar, s_xln, s_xrs, s_xn1, s_xn2, s_xsc = (
            sem(n) for n in ("x_stats", "x_moments", "x_var", "x_ln", "x_rstd0", "x_newton1", "x_newton2", "x_scale"))
        s_qf, s_qhi, s_qlo, s_khi, s_klo = (sem(n) for n in ("q_f", "q_hi", "q_lo", "k_hi", "k_lo"))
        s_vpad = sem("v_pad_ready")
        s_sn, s_max, s_nmhi, s_nmlo = sem("scores_qk"), sem("max_done"), sem("negmax_hi"), sem("negmax_lo")
        s_mt, s_mrows = sem("max_transposed"), sem("max_rows")
        s_st, s_exp = sem("scores_kq"), sem("exp_done")
        s_pv = sem("pv_done")
        s_dln, s_dinv, s_t1, s_t2, s_att, s_x2 = (
            sem(n) for n in ("den_ln", "den_inv0", "den_newton1", "den_inv", "attn_out", "x2_ready"))
        s_yst, s_ymv, s_yvar, s_yln, s_yrs, s_yn1, s_yn2, s_ysc = (
            sem(n) for n in ("y_stats", "y_moments", "y_var", "y_ln", "y_rstd0", "y_newton1", "y_newton2", "y_scale"))
        s_x2n, s_logit = sem("x2n_ready"), sem("logit_ready")
        s_nabs, s_ecoef, s_e1, s_wtop, s_c1, s_coef = (
            sem(n) for n in ("neg_abs", "coef_exp", "coef_sum", "top_weight", "coef_1", "coefs_ready"))
        s_xt, s_xthi, s_xtlo = sem("xt_transposed"), sem("xt_hi_ready"), sem("xt_lo_ready")
        s_h, s_r, s_l, s_a, s_ahi, s_alo = (
            sem(n) for n in ("h_ready", "relu_ready", "leaky_ready", "square_ready", "a_hi_ready", "a_lo_ready"))
        s_f2 = sem("a_buffers_free")
        s_o, s_ofree, s_resid, s_y1, s_y2 = (
            sem(n) for n in ("expert_out", "expert_out_free", "resid_ready", "y1_ready", "y2_ready"))

        def wait(eng, s, value):
            if not (isinstance(value, int) and value <= 0):
                eng.wait_ge(s, value)

        def wait_alone(eng, s, value):
            if not (isinstance(value, int) and value <= 0):
                eng.wait_ge(s, value)
                if not isinstance(value, int):
                    eng.sem_inc(s_passed, 1)

        def run_steps(eng, step):
            step(0, ffn=False, last=False)
            with eng.Fori(1, STEPS - 1) as i:
                step(i, ffn=True, last=False)
            step(STEPS - 1, ffn=True, last=True)

        block = stack.enter_context(nc.Block())

        @block.sync
        def _(sp):
            def batch(t, u, j):
                at = t[2 * u + j] if isinstance(u, int) else t[bass.ds(u * 2 + j, 1)].rearrange("o p n -> (o p) n")
                return at

            def load(u, j):
                m = u * 2 + j
                wait_alone(sp, s_qf, m - 1)
                sp.dma_start(x_raw[j][:, :], batch(x, u, j)).then_inc(s_x[j], 16)
                wait_alone(sp, s_khi, m - 1)
                wait_alone(sp, s_klo, m - 1)
                sp.dma_start(kv_raw[j][:, :], batch(ctx_kv, u, j)).then_inc(s_kv[j], 16)

            def load_v(u, j):
                wait_alone(sp, s_vpad, u * 2 + j - 1)
                sp.dma_start(v_raw[j][:, :, :], batch(ctx_t, u, j).rearrange("(c p) n -> p c n", p=P)).then_inc(s_v[j], 16)

            def stack_k(u, j):
                m = u * 2 + j
                wait_alone(sp, s_kst[j], 96 * u)
                wait_alone(sp, s_khi, m + 1)
                sp.dma_start(k_scr[j][0], k_hi[j][:, :].bitcast(f32)).then_inc(s_kscr[j], 16)
                wait_alone(sp, s_klo, m + 1)
                sp.dma_start(k_scr[j][1], k_lo[j][:, :].bitcast(f32)).then_inc(s_kscr[j], 16)

            def stack_q(u, j):
                m = u * 2 + j
                wait_alone(sp, s_qst[j], 48 * u)
                wait_alone(sp, s_qhi, m + 1)
                sp.dma_start(q_scr[j][0], q_hi[j][:, :].bitcast(f32)).then_inc(s_qscr[j], 16)
                wait_alone(sp, s_qlo, m + 1)
                sp.dma_start(q_scr[j][1], q_lo[j][:, :].bitcast(f32)).then_inc(s_qscr[j], 16)

            def read_k(u, j):
                wait_alone(sp, s_st, 8 * (u * 2 + j) - 8)
                wait_alone(sp, s_kscr[j], 32 * u + 32)
                for e in range(2):
                    for blk, part in enumerate((0, 1, 0)):
                        src = k_scr[j][part].rearrange("(g e r) n -> e r g n", g=PAIRS, e=2)[e]
                        row = 32 * blk + HD * e
                        sp.dma_start(k_st[j][row:row + HD, e, :, :].bitcast(f32), src).then_inc(s_kst[j], 16)

            def read_q(u, j):
                wait_alone(sp, s_st, 8 * (u * 2 + j) - 8)
                wait_alone(sp, s_qscr[j], 32 * u + 32)
                for blk, part in enumerate((0, 0, 1)):
                    src = q_scr[j][part].rearrange("(g r) n -> r g n", g=PAIRS)
                    sp.dma_start(q_st[j][32 * blk:32 * blk + 32, :, :].bitcast(f32), src).then_inc(s_qst[j], 16)

            def keep(u, j):
                wait_alone(sp, s_x2, u * 2 + j - 1)
                sp.dma_start(x_keep[j][:, :], batch(x, u, j)).then_inc(s_keep[j], 16)

            def store(g):
                wait_alone(sp, s_y2, g + 1)
                dst = (out[2 * g:2 * g + 2] if isinstance(g, int) else out[bass.ds(g * 2, 2)]).rearrange("t p n -> p t n")
                sp.dma_start(dst, y2[:, :, :]).then_inc(s_out, 16)

            load(0, 0)
            sp.dma_start(cst[:, :], consts).then_inc(s_cst, 16)
            load(0, 1)
            stack_k(0, 0)
            stack_q(0, 0)
            sp.wait_ge(s_zero[0], 1)
            read_k(0, 0)
            read_q(0, 0)
            stack_k(0, 1)
            stack_q(0, 1)
            sp.wait_ge(s_zero[1], 1)
            read_k(0, 1)
            read_q(0, 1)
            load_v(0, 0)
            load(1, 0)
            load_v(0, 1)
            load(1, 1)
            keep(0, 0)
            keep(0, 1)
            sp.dma_start(w_raw[0][:, :].rearrange("p (k n) -> p k n", k=KC),
                         w_fc_t.rearrange("(k p) n -> p k n", p=P)).then_inc(s_wraw[0], 16)
            sp.dma_start(w_raw[1][:, :].rearrange("p (c n) -> p c n", c=CHUNKS),
                         w_proj_t.rearrange("(c p) n -> p c n", p=P)).then_inc(s_wraw[1], 16)

            def step(i, ffn, last):
                for j in range(2):
                    if ffn:
                        if not last:
                            load(i + 1, j)
                        keep(i, j)
                    if not last:
                        stack_k(i + 1, j)
                        stack_q(i + 1, j)
                        read_k(i + 1, j)
                        read_q(i + 1, j)
                        load_v(i + 1, j)
                if ffn:
                    store(i - 1)

            run_steps(sp, step)
            store(STEPS - 1)
            sp.wait_ge(s_out, 16 * STEPS)

        @block.gpsimd
        def _(pool):
            pool.memset(k_st[1][:, :, :, :].bitcast(f32), 0.0).then_inc(s_zero[1], 1)
            pool.memset(v_pad[0][:, :, :], 0.0).then_inc(s_vzero, 1)
            pool.memset(v_pad[1][:, :, :], 0.0).then_inc(s_vzero, 1)

            def split_k(u, j):
                m = u * 2 + j
                pool.wait_ge(s_khi, m + 1)
                wait(pool, s_kscr[j], 32 * u)
                pool.tensor_tensor(k_lo[j][:, :], kv_raw[j][:, :], k_hi[j][:, :].bitcast(f32), ALU.subtract).then_inc(s_klo, 1)

            def pad_v(u, j):
                m = u * 2 + j
                pool.wait_ge(s_v[j], 16 * u + 16)
                wait_alone(pool, s_pv, 2 * m - 2)
                src = v_raw[j][:, :, :].rearrange("p c (g n) -> p (c g) n", g=PAIRS)
                pool.tensor_copy(v_pad[j][:, :, 0:16], src[:, :, 0:16])
                pool.tensor_copy(v_pad[j][:, :, 48:64], src[:, :, 16:32]).then_inc(s_vpad, 1)

            def split_w(w, n):
                at = slice(n * WPIECE, (n + 1) * WPIECE)
                pool.wait_ge(s_whi, w * N_WPIECES + n + 1)
                pool.tensor_tensor(w_lo[w][:, at], w_raw[w][:, at], w_hi[w][:, at].bitcast(f32), ALU.subtract).then_inc(s_wlo_p, 1)

            def square(g, c):
                pool.wait_ge(s_l, g * 16 + (c + 1))
                pool.tensor_tensor(a_buf[c % 2][:, :], l_buf[c % 2][:, :], l_buf[c % 2][:, :], ALU.mult).then_inc(s_a, 1)

            split_k(0, 0)
            split_k(0, 1)
            pool.wait_ge(s_vzero, 2)
            pad_v(0, 0)
            pad_v(0, 1)

            def step(i, ffn, last):
                for j in range(2):
                    if ffn:
                        square(i - 1, CH * j + 0)
                        square(i - 1, CH * j + 1)
                        square(i - 1, CH * j + 2)
                    if not last:
                        split_k(i + 1, j)
                    if ffn:
                        square(i - 1, CH * j + 3)
                    if not ffn:
                        split_w(j, 0)
                        split_w(j, 1)
                    if ffn:
                        square(i - 1, CH * j + 4)
                    if not ffn:
                        split_w(j, 2)
                    if ffn:
                        square(i - 1, CH * j + 5)
                        square(i - 1, CH * j + 6)
                    if not last:
                        pad_v(i + 1, j)
                    if ffn:
                        square(i - 1, CH * j + 7)
                    if not ffn:
                        split_w(j, 3)

            run_steps(pool, step)
            for c in range(CHUNKS):
                square(STEPS - 1, c)

        @block.scalar
        def _(act):
            def k_part_hi(u, j):
                m = u * 2 + j
                act.wait_ge(s_kv[j], 16 * u + 16)
                wait(act, s_kscr[j], 32 * u)
                act.activation(k_hi[j][:, :], kv_raw[j][:, :], ACT.Copy).then_inc(s_khi, 1)

            def q_part_hi(u, j):
                m = u * 2 + j
                act.wait_ge(s_qf, m + 1)
                wait(act, s_qscr[j], 32 * u)
                act.activation(q_hi[j][:, :], q_f[j][:, :], ACT.Copy).then_inc(s_qhi, 1)

            def x_ln(u, j):
                act.wait_ge(s_xvar, u * 2 + j + 1)
                act.activation(xln[j][:, :], xvar[j][:, :], ACT.Ln).then_inc(s_xln, 1)

            def x_rstd(u, j):
                act.wait_ge(s_xln, u * 2 + j + 1)
                act.activation(xrs[j][:, :], xln[j][:, :], ACT.Exp, scale=-0.5).then_inc(s_xrs, 1)

            def y_ln(i, j):
                act.wait_ge(s_yvar, i * 2 + (j + 1))
                act.activation(yln[j][:, :], yvar[j][:, :], ACT.Ln).then_inc(s_yln, 1)

            def y_rstd(i, j):
                act.wait_ge(s_yln, i * 2 + (j + 1))
                act.activation(yrs[j][:, :], yln[j][:, :], ACT.Exp, scale=-0.5).then_inc(s_yrs, 1)

            def max_rows(i, j):
                b = i * 2 + j
                act.wait_ge(s_mt, b + 1)
                act.wait_ge(s_qst[j], 48 * i + 48)
                act.activation(q_st[j][MBLK:STACK, :, :],
                               misc[0:2 * HEADS, 0:DIM].unsqueeze(1).to_broadcast([2 * HEADS, PAIRS, DIM]),
                               ACT.Copy).then_inc(s_mrows, 1)

            def exp(i, j, k):
                b = i * 2 + j
                act.wait_ge(s_st, 8 * b + (k + 1))
                wait(act, s_pv, b * 2 - 1 if k < 4 else b * 2)
                act.activation(probs[HEAD_ORDER[k]][:, :, :], stp[k % 2][:, :].rearrange("p (c n) -> p c n", c=KC),
                               ACT.Exp).then_inc(s_exp, 1)

            def den_ln(i, j):
                b = i * 2 + j
                act.wait_ge(s_pv, b * 2 + 2)
                wait(act, s_t2, b)
                act.activation(dln[:, :], pv[:, DIM:2 * DIM], ACT.Ln).then_inc(s_dln, 1)

            def den_inverse(i, j):
                act.wait_ge(s_dln, i * 2 + (j + 1))
                act.activation(dinv[:, :], dln[:, :], ACT.Exp, scale=-1.0).then_inc(s_dinv, 1)

            def relu(g, c):
                act.wait_ge(s_h, g * 16 + (c + 1))
                act.activation(r_buf[c % 2][:, :], hps[c % 2][:, 0:2 * P], ACT.Relu, scale=0.5).then_inc(s_r, 1)

            def square_hi(g, c):
                act.wait_ge(s_l, g * 16 + (c + 1))
                act.wait_ge(s_f2, g * 16 + (c + 1))
                act.activation(a_hi[c % NA][:, :], l_buf[c % 2][:, :], ACT.Square).then_inc(s_ahi, 1)

            def coef_exp(g):
                act.wait_ge(s_nabs, g + 1)
                act.activation(ecoef[:, :], nabs[:, :], ACT.Exp).then_inc(s_ecoef, 1)

            def xt_part_hi(i):
                act.wait_ge(s_xt, i + 1)
                act.activation(xt_hi[:, :, :], misc[:, :].rearrange("p (c n) -> p c n", c=KC), ACT.Copy).then_inc(s_xthi, 1)

            def split_w(w, n):
                at = slice(n * WPIECE, (n + 1) * WPIECE)
                act.wait_ge(s_wraw[w], 16)
                act.activation(w_hi[w][:, at], w_raw[w][:, at], ACT.Copy).then_inc(s_whi, 1)

            def pick_rows(j):
                act.activation(k_st[j][MBLK:STACK, :, :, :].rearrange("p e g n -> p (e g) n"),
                               pick.unsqueeze(2).to_broadcast([2 * HEADS, HEADS, KEYS]), ACT.Copy).then_inc(s_pick, 1)

            act.preload_act_table_set("natural_log_exp_and_others")
            act.dma_start(len_i[:, :], k_len.partition_broadcast(P)).then_inc(s_len, 16)
            act.dma_start(wr[:, :, :], w_router.partition_broadcast(P)).then_inc(s_wr, 16)
            k_part_hi(0, 0)
            act.wait_ge(s_lenf, 1)
            act.activation(len_ln[:, :], len_f[:, :], ACT.Ln).then_inc(s_lenln, 1)
            x_ln(0, 0)
            x_rstd(0, 0)
            q_part_hi(0, 0)
            k_part_hi(0, 1)
            x_ln(0, 1)
            x_rstd(0, 1)
            q_part_hi(0, 1)
            act.wait_ge(s_cst, 16)
            for j in range(2):
                act.wait_ge(s_zero[j], 1)
                pick_rows(j)

            max_rows(0, 0)

            def step(i, ffn, last):
                for j in range(2):
                    ahead = not (last and j == 1)
                    if ffn:
                        relu(i - 1, CH * j + 0)
                    exp(i, j, 0)
                    exp(i, j, 1)
                    if ffn:
                        square_hi(i - 1, CH * j + 0)
                    if not last:
                        k_part_hi(i + 1, j)
                    if ffn:
                        relu(i - 1, CH * j + 1)
                    exp(i, j, 2)
                    if ffn and j == 0:
                        coef_exp(i - 1)
                    exp(i, j, 3)
                    if not last:
                        x_ln(i + 1, j)
                    if ffn:
                        relu(i - 1, CH * j + 2)
                        square_hi(i - 1, CH * j + 1)
                    if not last:
                        x_rstd(i + 1, j)
                    exp(i, j, 4)
                    if ffn:
                        square_hi(i - 1, CH * j + 2)
                        relu(i - 1, CH * j + 3)
                    exp(i, j, 5)
                    exp(i, j, 6)
                    exp(i, j, 7)
                    if not ffn:
                        split_w(j, 0)
                    if not last:
                        q_part_hi(i + 1, j)
                    if ffn:
                        square_hi(i - 1, CH * j + 3)
                        relu(i - 1, CH * j + 4)
                    if not ffn:
                        split_w(j, 1)
                    if ffn:
                        relu(i - 1, CH * j + 5)
                        square_hi(i - 1, CH * j + 4)
                    den_ln(i, j)
                    den_inverse(i, j)
                    if ffn:
                        relu(i - 1, CH * j + 6)
                    if not ffn:
                        split_w(j, 2)
                    if ffn:
                        square_hi(i - 1, CH * j + 5)
                    y_ln(i, j)
                    if ffn:
                        square_hi(i - 1, CH * j + 6)
                    y_rstd(i, j)
                    if ffn:
                        relu(i - 1, CH * j + 7)
                    if ahead:
                        max_rows(i + j, 1 - j)
                    if not ffn:
                        split_w(j, 3)
                    if ffn:
                        square_hi(i - 1, CH * j + 7)
                xt_part_hi(i)

            run_steps(act, step)
            g = STEPS - 1
            for c in range(CHUNKS):
                relu(g, c)
                if c > 0:
                    square_hi(g, c - 1)
                if c == 0:
                    coef_exp(g)
            square_hi(g, CHUNKS - 1)

        @block.vector
        def _(dve):
            def moments(stage, m, src, st, mv, var, s_st_, s_mv_, s_var_):
                if stage == 0:
                    dve.bn_stats(st[:, :], src).then_inc(s_st_, 1)
                elif stage == 1:
                    wait_alone(dve, s_st_, m + 1)
                    dve.bn_aggr(mv[:, :], st[:, :]).then_inc(s_mv_, 1)
                else:
                    dve.wait_ge(s_mv_, m + 1)
                    dve.tensor_scalar(var[:, :], mv[:, 1:2], EPS, None, ALU.add).then_inc(s_var_, 1)

            def newton(stage, m, var, rs, n1, n2, sc, extra, s_rs_, s_n1_, s_n2_, s_sc_):
                if stage == 0:
                    dve.wait_ge(s_rs_, m + 1)
                    dve.scalar_tensor_tensor(n1[:, :], rs[:, :], rs[:, 0:1], var[:, :], ALU.mult, ALU.mult).then_inc(s_n1_, 1)
                elif stage == 1:
                    dve.wait_ge(s_n1_, m + 1)
                    dve.tensor_scalar(n2[:, :], n1[:, :], -0.5, 1.5, ALU.mult, ALU.add).then_inc(s_n2_, 1)
                else:
                    dve.wait_ge(s_n2_, m + 1)
                    dve.scalar_tensor_tensor(sc[:, :], n2[:, :], extra, rs[:, :], ALU.mult, ALU.mult).then_inc(s_sc_, 1)

            def x_moments(u, j, stage):
                if stage == 0:
                    dve.wait_ge(s_x[j], 16 * u + 16)
                moments(stage, u * 2 + j, x_raw[j][:, :], xst[j], xmv[j], xvar[j], s_xst, s_xmv, s_xvar)

            def x_newton(u, j, stage):
                m = u * 2 + j
                sc_b = scale_b[:, m:m + 1] if isinstance(u, int) else scale_b[:, bass.ds(m, 1)]
                newton(stage, m, xvar[j], xrs[j], xn1[j], xn2[j], xsc[j], sc_b, s_xrs, s_xn1, s_xn2, s_xsc)

            def q_normalise(u, j):
                dve.wait_ge(s_xsc, u * 2 + j + 1)
                dve.tensor_scalar(q_f[j][:, :], x_raw[j][:, :], xmv[j][:, 0:1], xsc[j][:, 0:1],
                                  ALU.subtract, ALU.mult).then_inc(s_qf, 1)

            def q_part_lo(u, j):
                m = u * 2 + j
                dve.wait_ge(s_qhi, m + 1)
                wait(dve, s_qscr[j], 32 * u)
                dve.tensor_tensor(q_lo[j][:, :], q_f[j][:, :], q_hi[j][:, :].bitcast(f32), ALU.subtract).then_inc(s_qlo, 1)

            def row_max(n, j, h, scores=sn):
                dve.wait_ge(s_sn, 8 * n + (h + 1))
                dve.tensor_reduce(negm[j][:, :, h], scores[:, :].rearrange("p (c n) -> p c n", c=KC),
                                  AX.X, ALU.max, negate=True).then_inc(s_max, 1)

            def split_max_hi(n, j):
                dve.wait_ge(s_max, 8 * n + 8)
                dve.tensor_copy(nm_r[j][:, :, 0, :], negm[j][:, :, :]).then_inc(s_nmhi, 1)

            def split_max_lo(n, j):
                dve.wait_ge(s_nmhi, n + 1)
                dve.tensor_tensor(nm_r[j][:, :, 1, :], negm[j][:, :, :], nm_r[j][:, :, 0, :].bitcast(f32),
                                  ALU.subtract).then_inc(s_nmlo, 1)

            def den_newton(i, j):
                dve.wait_ge(s_dinv, i * 2 + (j + 1))
                dve.tensor_tensor(t1[:, :], pv[:, DIM:2 * DIM], dinv[:, :], ALU.mult).then_inc(s_t1, 1)

            def den_inv(i, j):
                dve.wait_ge(s_t1, i * 2 + (j + 1))
                dve.scalar_tensor_tensor(t2[:, :], t1[:, :], -2.0, dinv[:, :], ALU.add, ALU.mult).then_inc(s_t2, 1)

            def attention_out(i, j):
                dve.wait_ge(s_t2, i * 2 + (j + 1))
                dve.tensor_tensor(att[:, :], pv[:, 0:DIM], t2[:, :], ALU.mult).then_inc(s_att, 1)

            def x2_sum(i, j):
                dve.wait_ge(s_att, i * 2 + (j + 1))
                dve.wait_ge(s_keep[j], 16 * i + 16)
                dve.tensor_tensor(x2[j][:, :], x_keep[j][:, :], att[:, :], ALU.subtract).then_inc(s_x2, 1)

            def x2_moments(i, j, stage):
                if stage == 0:
                    dve.wait_ge(s_x2, i * 2 + (j + 1))
                moments(stage, i * 2 + j, x2[j][:, :], yst[j], ymv[j], yvar[j], s_yst, s_ymv, s_yvar)

            def x2_newton(i, j, stage):
                newton(stage, i * 2 + j, yvar[j], yrs[j], yn1[j], yn2[j], ysc[j], 1.0, s_yrs, s_yn1, s_yn2, s_ysc)

            def x2_normalise(i, j):
                dve.wait_ge(s_ysc, i * 2 + (j + 1))
                dve.tensor_scalar(x2n[j][:, :], x2[j][:, :], ymv[j][:, 0:1], ysc[j][:, 0:1],
                                  ALU.subtract, ALU.mult).then_inc(s_x2n, 1)

            def router(i, j):
                dve.wait_ge(s_x2n, i * 2 + (j + 1))
                dve.scalar_tensor_tensor(dot_out[:, :], x2n[j][:, :], 1.0, wr_diff[:, :], ALU.mult, ALU.mult,
                                         accum_out=logit[:, j:j + 1]).then_inc(s_logit, 1)

            def neg_logit(g):
                dve.wait_ge(s_logit, g * 2 + 2)
                dve.tensor_scalar(e1[:, :], logit[:, :], -1.0, None, ALU.mult).then_inc(s_e1, 1)

            def neg_abs(g):
                dve.wait_ge(s_e1, g * 2 + 1)
                dve.tensor_tensor(nabs[:, :], logit[:, :], e1[:, :], ALU.min).then_inc(s_nabs, 1)

            def coef_sum(g):
                dve.wait_ge(s_ecoef, g + 1)
                dve.tensor_scalar(e1[:, :], ecoef[:, :], 1.0, None, ALU.add).then_inc(s_e1, 1)

            def top_weight(g):
                dve.wait_ge(s_e1, g * 2 + 2)
                dve.reciprocal(wtop[:, :], e1[:, :]).then_inc(s_wtop, 1)

            def coefs(g):
                dve.wait_ge(s_wtop, g + 1)
                dve.scalar_tensor_tensor(coef[1][:, :], logit[:, :], 0.0, wtop[:, :], ALU.is_gt, ALU.mult).then_inc(s_c1, 1)
                dve.scalar_tensor_tensor(coef[0][:, :], logit[:, :], 0.0, wtop[:, :], ALU.is_le, ALU.mult).then_inc(s_coef, 1)

            def residual_copy(g):
                dve.wait_ge(s_x2, g * 2 + 2)
                for t in range(2):
                    last = dve.tensor_copy(resid[:, t, :], x2[t][:, :])
                last.then_inc(s_resid, 1)

            def leaky(g, c):
                dve.wait_ge(s_r, g * 16 + (c + 1))
                dve.scalar_tensor_tensor(l_buf[c % 2][:, :], hps[c % 2][:, 0:2 * P], 0.5, r_buf[c % 2][:, :],
                                         ALU.mult, ALU.add).then_inc(s_l, 1)

            def square_lo(g, c):
                dve.wait_ge(s_a, g * 16 + (c + 1))
                dve.wait_ge(s_ahi, g * 16 + (c + 1))
                dve.tensor_tensor(a_lo[c % NA][:, :], a_buf[c % 2][:, :], a_hi[c % NA][:, :].bitcast(f32),
                                  ALU.subtract).then_inc(s_alo, 1)

            def expert_out(g, e):
                dve.wait_ge(s_o, g * 2 + (e + 1))
                if e == 0:
                    dve.wait_ge(s_coef, g + 1)
                    dve.wait_ge(s_resid, g + 1)
                    for t in range(2):
                        last = dve.scalar_tensor_tensor(y1[:, t, :], ops_[:, t * DIM:(t + 1) * DIM], coef[0][:, t:t + 1],
                                                        resid[:, t, :], ALU.mult, ALU.add)
                    last.then_inc(s_ofree, 1)
                else:
                    dve.wait_ge(s_c1, g + 1)
                    dve.wait_ge(s_ofree, g * 2 + 1)
                    wait(dve, s_out, 16 * g)
                    for t in range(2):
                        last = dve.scalar_tensor_tensor(y2[:, t, :], ops_[:, t * DIM:(t + 1) * DIM], coef[1][:, t:t + 1],
                                                        y1[:, t, :], ALU.mult, ALU.add)
                    last.then_inc(s_ofree, 1)
                    dve.wait_ge(s_ofree, g * 2 + 2)
                    dve.sem_inc(s_y2, 1)

            def xt_part_lo(i):
                dve.wait_ge(s_xthi, i + 1)
                dve.tensor_tensor(xt_lo[:, :, :], misc[:, :].rearrange("p (c n) -> p c n", c=KC),
                                  xt_hi[:, :, :].bitcast(f32), ALU.subtract).then_inc(s_xtlo, 1)

            dve.memset(k_st[0][:, :, :, :].bitcast(f32), 0.0).then_inc(s_zero[0], 1)
            for stage in range(3):
                x_moments(0, 0, stage)
            dve.wait_ge(s_len, 16)
            dve.tensor_copy(len_f[:, :], len_i[:, :]).then_inc(s_lenf, 1)
            dve.wait_ge(s_lenln, 1)
            dve.tensor_scalar(scale_b[:, :], len_ln[:, :], SCORE_SCALE, None, ALU.mult).then_inc(s_scale, 1)
            dve.wait_ge(s_scale, 1)
            for stage in range(3):
                x_newton(0, 0, stage)
            q_normalise(0, 0)
            for stage in range(3):
                x_moments(0, 1, stage)
            q_part_lo(0, 0)
            for stage in range(3):
                x_newton(0, 1, stage)
            q_normalise(0, 1)
            q_part_lo(0, 1)
            dve.wait_ge(s_wr, 16)
            dve.tensor_tensor(wr_diff[:, :], wr[:, 1, :], wr[:, 0, :], ALU.subtract).then_inc(s_wrd, 1)
            dve.wait_ge(s_wrd, 1)
            for h in range(HEADS):
                row_max(0, 0, h, scores=sn_first[h % 2])
            split_max_hi(0, 0)
            split_max_lo(0, 0)

            def step(i, ffn, last):
                for j in range(2):
                    ahead = not (last and j == 1)
                    if ffn and j == 0:
                        residual_copy(i - 1)
                    if ffn:
                        leaky(i - 1, CH * j + 0)
                    if ffn and j == 0:
                        neg_logit(i - 1)
                    if ffn and j == 1:
                        square_lo(i - 1, CH * j + -1)
                    if ffn and j == 0:
                        neg_abs(i - 1)
                    if not last:
                        x_moments(i + 1, j, 0)
                    if ffn:
                        square_lo(i - 1, CH * j + 0)
                    if not last:
                        x_moments(i + 1, j, 1)
                    if ahead:
                        row_max(i * 2 + (j + 1), 1 - j, 0)
                    if not last:
                        x_moments(i + 1, j, 2)
                    if ffn and j == 0:
                        coef_sum(i - 1)
                    if ffn:
                        leaky(i - 1, CH * j + 1)
                        leaky(i - 1, CH * j + 2)
                        square_lo(i - 1, CH * j + 1)
                    if not last:
                        x_newton(i + 1, j, 0)
                    if ffn and j == 0:
                        top_weight(i - 1)
                    if not last:
                        x_newton(i + 1, j, 1)
                        x_newton(i + 1, j, 2)
                    if ffn and j == 0:
                        coefs(i - 1)
                    if ffn:
                        square_lo(i - 1, CH * j + 2)
                    if ffn and j == 1:
                        expert_out(i - 1, 0)
                    if ahead:
                        row_max(i * 2 + (j + 1), 1 - j, 1)
                    if ffn:
                        leaky(i - 1, CH * j + 3)
                    if not last:
                        q_normalise(i + 1, j)
                    if ahead:
                        row_max(i * 2 + (j + 1), 1 - j, 2)
                        row_max(i * 2 + (j + 1), 1 - j, 3)
                    if ffn:
                        leaky(i - 1, CH * j + 4)
                        square_lo(i - 1, CH * j + 3)
                    if not last:
                        q_part_lo(i + 1, j)
                    if ahead:
                        row_max(i * 2 + (j + 1), 1 - j, 4)
                    if ffn:
                        leaky(i - 1, CH * j + 5)
                        square_lo(i - 1, CH * j + 4)
                    if ahead:
                        row_max(i * 2 + (j + 1), 1 - j, 5)
                    den_newton(i, j)
                    den_inv(i, j)
                    attention_out(i, j)
                    x2_sum(i, j)
                    if ahead:
                        row_max(i * 2 + (j + 1), 1 - j, 6)
                    x2_moments(i, j, 0)
                    x2_moments(i, j, 1)
                    if ffn:
                        leaky(i - 1, CH * j + 6)
                    x2_moments(i, j, 2)
                    if ahead:
                        row_max(i * 2 + (j + 1), 1 - j, 7)
                    if ffn:
                        square_lo(i - 1, CH * j + 5)
                    x2_newton(i, j, 0)
                    if ahead:
                        split_max_hi(i * 2 + (j + 1), 1 - j)
                    x2_newton(i, j, 1)
                    if ahead:
                        split_max_lo(i * 2 + (j + 1), 1 - j)
                    x2_newton(i, j, 2)
                    if ffn:
                        square_lo(i - 1, CH * j + 6)
                    x2_normalise(i, j)
                    if ffn:
                        leaky(i - 1, CH * j + 7)
                    router(i, j)
                if ffn:
                    square_lo(i - 1, CHUNKS - 1)
                xt_part_lo(i)
                if ffn:
                    expert_out(i - 1, 1)

            run_steps(dve, step)
            g = STEPS - 1
            for c in range(CHUNKS):
                leaky(g, c)
                if c == 0:
                    neg_logit(g)
                    neg_abs(g)
                    residual_copy(g)
                if c == 1:
                    coef_sum(g)
                    top_weight(g)
                    coefs(g)
                if c > 0:
                    square_lo(g, c - 1)
                if c == CH + LAG - 1:
                    expert_out(g, 0)
            square_lo(g, CHUNKS - 1)
            expert_out(g, 1)

        @block.tensor
        def _(pe):
            def scores_qk(i, j, h, scores=sn, behind=0):
                b = i * 2 + j
                if h == 0:
                    pe.wait_ge(s_qst[j], 48 * i + 48)
                    pe.wait_ge(s_kst[j], 96 * i + 96)
                wait(pe, s_max, 8 * b + (h - behind))
                for qc in range(KC):
                    last = pe.matmul(scores[:, qc * KEYS:(qc + 1) * KEYS],
                                     q_st[j][0:MBLK, h // 2, qc * P:(qc + 1) * P], k_st[j][0:MBLK, h % 2, h // 2, :],
                                     start=(qc == 0), stop=True, skip_group_check=True)
                last.then_inc(s_sn, 1)

            def max_transpose(i, j):
                b = i * 2 + j
                pe.wait_ge(s_nmlo, b + 1)
                wait(pe, s_mrows, b)
                wait(pe, s_xtlo, i - (1 - j))
                for qc in range(KC):
                    last = pe.transpose(misc[0:2 * HEADS, qc * P:(qc + 1) * P],
                                        nm_r[j][:, qc, :, :].rearrange("p a h -> p (a h)").bitcast(f32), ident)
                last.then_inc(s_mt, 1)

            def scores_kq(i, j, k):
                b, h = i * 2 + j, HEAD_ORDER[k]
                if k == 0:
                    pe.wait_ge(s_mrows, b + 1)
                wait(pe, s_exp, 8 * b + (k - 1))
                for kc in range(KC):
                    last = pe.matmul(stp[k % 2][:, kc * DIM:(kc + 1) * DIM],
                                     k_st[j][0:STACK, h % 2, h // 2, kc * P:(kc + 1) * P], q_st[j][0:STACK, h // 2, :],
                                     start=(kc == 0), stop=True, skip_group_check=True)
                last.then_inc(s_st, 1)

            def values(i, j, e, kc, den):
                b = i * 2 + j
                if kc == 0 and den == 0:
                    pe.wait_ge(s_exp, 8 * b + 4 + 4 * e)
                    if e == 0:
                        pe.wait_ge(s_vpad, b + 1)
                        wait(pe, s_att, b)
                for g in range(PAIRS):
                    lhs = ones_v[e] if den else v_pad[j][:, kc * PAIRS + g, 32 * e:32 * e + 32]
                    last = pe.matmul(pv[32 * g:32 * g + 32, den * DIM:(den + 1) * DIM], lhs, probs[2 * g + e][:, kc, :],
                                     start=(e == 0 and kc == 0 and den == 0), stop=(e == 1 and kc == 1),
                                     skip_group_check=True)
                if kc == 1 and den == 1:
                    last.then_inc(s_pv, 1)

            def ffn1(g, c):
                if c >= 2:
                    pe.wait_ge(s_l, g * 16 + (c - 1))
                if c == 0:
                    pe.wait_ge(s_xthi, g + 1)
                    pe.wait_ge(s_xtlo, g + 1)
                for kc in range(KC):
                    for w, xt in ((0, xt_hi), (1, xt_hi), (0, xt_lo)):
                        last = pe.matmul(hps[c % 2][:, 0:2 * P], wfc[w][:, kc, c * P:(c + 1) * P], xt[:, kc, :],
                                         start=(kc == 0 and w == 0 and xt is xt_hi), stop=(kc == KC - 1 and xt is xt_lo))
                last.then_inc(s_h, 1)

            def ffn2(g, c):
                pe.wait_ge(s_ahi, g * 16 + (c + 1))
                if c % CH == 0:
                    wait(pe, s_ofree, g * 2 + c // CH)
                for part in range(3):
                    if part == 2:
                        pe.wait_ge(s_alo, g * 16 + (c + 1))
                    for t in range(2):
                        a, w = ((a_hi, 0), (a_hi, 1), (a_lo, 0))[part]
                        last = pe.matmul(ops_[:, t * DIM:(t + 1) * DIM], a[c % NA][:, t * P:(t + 1) * P], wproj[w][:, c, :],
                                         start=(c % CH == 0 and part == 0 and t == 0), stop=(c % CH == CH - 1 and part == 2),
                                         skip_group_check=True)
                last.then_inc(s_f2, 1)
                if c % CH == CH - 1:
                    pe.wait_ge(s_f2, g * 16 + (c + 1 + NA))
                    pe.sem_inc(s_o, 1)

            def x_transpose(i, last):
                pe.wait_ge(s_x2n, i * 2 + 2)
                pe.wait_ge(s_mrows, i * 2 + (2 if last else 3))
                for t in range(2):
                    for kc in range(KC):
                        last = pe.transpose(misc[:, kc * 2 * P + t * P:kc * 2 * P + (t + 1) * P],
                                            x2n[t][:, kc * P:(kc + 1) * P], ident)
                last.then_inc(s_xt, 1)

            pe.sem_inc(s_f2, NA)
            pe.wait_ge(s_cst, 16)
            for h in range(HEADS):
                scores_qk(0, 0, h, scores=sn_first[h % 2], behind=1)
            max_transpose(0, 0)
            pe.wait_ge(s_pick, 2)

            def step(i, ffn, last):
                for j in range(2):
                    ahead = not (last and j == 1)
                    if ffn:
                        ffn1(i - 1, CH * j + 0)
                    scores_kq(i, j, 0)
                    scores_kq(i, j, 1)
                    if ffn:
                        ffn1(i - 1, CH * j + 1)
                    if ffn and j == 1:
                        ffn2(i - 1, CH * j + 0 - LAG)
                    if ahead:
                        scores_qk(i + j, 1 - j, 0)
                    scores_kq(i, j, 2)
                    scores_kq(i, j, 3)
                    if ffn:
                        ffn1(i - 1, CH * j + 2)
                    if ahead:
                        scores_qk(i + j, 1 - j, 1)
                    if ffn and j == 1:
                        ffn2(i - 1, CH * j + 1 - LAG)
                    scores_kq(i, j, 4)
                    values(i, j, 0, 0, 0)
                    values(i, j, 0, 0, 1)
                    values(i, j, 0, 1, 0)
                    if ffn:
                        ffn1(i - 1, CH * j + 3)
                    scores_kq(i, j, 5)
                    scores_kq(i, j, 6)
                    if ffn:
                        ffn1(i - 1, CH * j + 4)
                    if ahead:
                        scores_qk(i + j, 1 - j, 2)
                    if ffn:
                        ffn2(i - 1, CH * j + 2 - LAG)
                    scores_kq(i, j, 7)
                    if ffn:
                        ffn2(i - 1, CH * j + 3 - LAG)
                    values(i, j, 0, 1, 1)
                    if ahead:
                        scores_qk(i + j, 1 - j, 3)
                    values(i, j, 1, 0, 0)
                    values(i, j, 1, 0, 1)
                    if ffn:
                        ffn1(i - 1, CH * j + 5)
                    values(i, j, 1, 1, 0)
                    if ahead:
                        scores_qk(i + j, 1 - j, 4)
                    values(i, j, 1, 1, 1)
                    if ffn:
                        ffn2(i - 1, CH * j + 4 - LAG)
                    if ahead:
                        scores_qk(i + j, 1 - j, 5)
                    if ffn:
                        ffn1(i - 1, CH * j + 6)
                        ffn2(i - 1, CH * j + 5 - LAG)
                    if ahead:
                        scores_qk(i + j, 1 - j, 6)
                    if ffn:
                        ffn2(i - 1, CH * j + 6 - LAG)
                    if ahead:
                        scores_qk(i + j, 1 - j, 7)
                    if ffn:
                        ffn1(i - 1, CH * j + 7)
                        ffn2(i - 1, CH * j + 7 - LAG)
                    if ahead:
                        max_transpose(i + j, 1 - j)
                x_transpose(i, last)
                if ffn:
                    for c in range(CHUNKS - LAG, CHUNKS):
                        ffn2(i - 1, c)
                else:
                    pe.wait_ge(s_wlo_p, 2 * N_WPIECES)

            run_steps(pe, step)
            g = STEPS - 1
            for c in range(CHUNKS + LAG):
                if c < CHUNKS:
                    ffn1(g, c)
                if c >= LAG:
                    ffn2(g, c - LAG)


def kernel(**inputs):
    import numpy as np
    import concourse.bacc as bacc
    from concourse.bass_utils import run_bass_kernel_spmd

    ctx = inputs["ctx_2048"]
    consts = np.zeros((P, 200), np.float32)
    consts[:, 0:128] = np.eye(128, dtype=np.float32)
    for e in range(2):
        consts[:, 128 + 32 * e + HD * e:128 + 32 * e + HD * e + HD] = 1.0
    for part in range(2):
        for h in range(HEADS):
            consts[MBLK + HEADS * part + h, 192 + PAIRS * (h % 2) + h // 2] = 1.0
    arrays = {
        "x": np.ascontiguousarray(inputs["x"]),
        "ctx_kv": np.ascontiguousarray(ctx),
        "ctx_t": np.ascontiguousarray(np.transpose(ctx, (0, 2, 1))),
        "k_len": np.ascontiguousarray(inputs["itok_B_779_1933"]),
        "w_router": np.ascontiguousarray(inputs["L0_ffn_w_router"]),
        "w_fc_t": np.ascontiguousarray(np.transpose(inputs["L0_ffn_w_fc"], (2, 0, 1)).reshape(DIM, EXPERTS * HID)),
        "w_proj_t": np.ascontiguousarray(np.transpose(inputs["L0_ffn_w_proj"], (0, 2, 1)).reshape(EXPERTS * HID, DIM)),
        "consts": consts,
    }
    nc = bacc.Bacc("TRN2", target_bir_lowering=False, num_devices=1)
    aps = {n: nc.dram_tensor(n, a.shape, mybir.dt.from_np(a.dtype), kind="ExternalInput").ap() for n, a in arrays.items()}
    out = nc.dram_tensor("out", (B, ROWS, DIM), mybir.dt.float32, kind="ExternalOutput").ap()
    build(nc, aps["x"], aps["ctx_kv"], aps["ctx_t"], aps["k_len"], aps["w_router"], aps["w_fc_t"], aps["w_proj_t"],
          aps["consts"], out)
    r = run_bass_kernel_spmd(nc, [arrays], core_ids=[0])
    return r.results[0]["out"]
```

```python
import concourse.bass as bass
from concourse import mybir
from contextlib import ExitStack
from math import log

B, ROWS, DIM = 8, 128, 256
HEADS, HD = 8, 16
PAIRS = HEADS // 2
KEYS = DIM
HID, EXPERTS = 1024, 2
P = 128
KC = DIM // P
CH = HID // P
CHUNKS = EXPERTS * CH
STEPS = B // 2
SCORE_SCALE = 1.0 / (64 ** 0.5 * log(20))
EPS = 1e-5
MBLK = 96
STACK = MBLK + 2 * HEADS
HEAD_ORDER = [0, 2, 4, 6, 1, 3, 5, 7]
LAG = 3
NA = 8
WPIECE = 1024
N_WPIECES = CHUNKS * DIM // WPIECE


def build(nc, x, ctx_kv, ctx_t, k_len, w_router, w_fc_t, w_proj_t, consts, out):
    f32, f32r, i32 = mybir.dt.float32, mybir.dt.float32r, mybir.dt.int32
    ALU, ACT, AX = mybir.AluOpType, mybir.ActivationFunctionType, mybir.AxisListType

    with ExitStack() as stack:
        def sb(name, shape, dt=f32):
            return stack.enter_context(nc.sbuf_tensor(name, shape, dt))

        def two(name, shape, dt=f32):
            return [sb(f"{name}{j}", shape, dt) for j in range(2)]

        def bank(name):
            return stack.enter_context(nc.psum_tensor(name, [P, 512], f32))

        def sem(name):
            return stack.enter_context(nc.semaphore(name))

        def sems(name):
            return [sem(f"{name}{j}") for j in range(2)]

        q_scr = [[nc.dram_tensor(f"q_scr{j}{h}", [P, DIM], f32, kind="Internal").ap() for h in "hl"] for j in range(2)]
        k_scr = [[nc.dram_tensor(f"k_scr{j}{h}", [P, DIM], f32, kind="Internal").ap() for h in "hl"] for j in range(2)]

        cst = sb("cst", [P, 200])
        ident = cst[:, 0:128]
        ones_v = [cst[:, 128 + 32 * e:160 + 32 * e] for e in range(2)]
        pick = cst[MBLK:STACK, 192:200]
        len_i = sb("len_i", [P, B], i32)
        len_f = sb("len_f", [P, B])
        len_ln = sb("len_ln", [P, B])
        scale_b = sb("scale_b", [P, B])
        wr = sb("wr", [P, EXPERTS, DIM])
        wr_diff = sb("wr_diff", [P, DIM])
        w_raw = [sb("wfc_raw", [P, CHUNKS * DIM]), sb("wproj_raw", [P, CHUNKS * DIM])]
        w_hi = [sb("wfc_hi", [P, CHUNKS * DIM], f32r), sb("wproj_hi", [P, CHUNKS * DIM], f32r)]
        w_lo = [sb("wfc_lo", [P, CHUNKS * DIM], f32r), sb("wproj_lo", [P, CHUNKS * DIM], f32r)]
        wfc = [w[:, :].rearrange("p (k n) -> p k n", k=KC) for w in (w_hi[0], w_lo[0])]
        wproj = [w[:, :].rearrange("p (c n) -> p c n", c=CHUNKS) for w in (w_hi[1], w_lo[1])]

        x_raw, x_keep, kv_raw = two("x_raw", [P, DIM]), two("x_keep", [P, DIM]), two("kv_raw", [P, DIM])
        v_raw = two("v_raw", [P, KC, ROWS])
        v_pad = two("v_pad", [P, KC * PAIRS, 64])
        xst, xmv, xvar = two("xst", [P, 6]), two("xmv", [P, 2]), two("xvar", [P, 1])
        xln, xrs, xn1, xn2, xsc = (two(n, [P, 1]) for n in ("xln", "xrs", "xn1", "xn2", "xsc"))
        q_f = two("q_f", [P, DIM])
        q_hi, q_lo, k_hi, k_lo = (two(n, [P, DIM], f32r) for n in ("q_hi", "q_lo", "k_hi", "k_lo"))
        q_st = two("q_st", [P, PAIRS, DIM], f32r)
        k_st = two("k_st", [P, 2, PAIRS, KEYS], f32r)
        negm = two("negm", [P, KC, HEADS])
        nm_r = two("nm_r", [P, KC, 2, HEADS], f32r)
        probs = [sb(f"probs{h}", [P, KC, DIM]) for h in range(HEADS)]
        dln, dinv, t1, t2, att = (sb(n, [P, DIM]) for n in ("dln", "dinv", "t1", "t2", "att"))
        x2, x2n = two("x2", [P, DIM]), two("x2n", [P, DIM])
        yst, ymv, yvar = two("yst", [P, 6]), two("ymv", [P, 2]), two("yvar", [P, 1])
        yln, yrs, yn1, yn2, ysc = (two(n, [P, 1]) for n in ("yln", "yrs", "yn1", "yn2", "ysc"))
        dot_out = sb("dot_out", [P, DIM])
        logit = sb("logit", [P, 2])
        nabs, ecoef, e1, wtop = (sb(n, [P, 2]) for n in ("nabs", "ecoef", "e1", "wtop"))
        coef = [sb(f"coef{e}", [P, 2]) for e in range(EXPERTS)]

        xt_hi, xt_lo = sb("xt_hi", [P, KC, 2 * P], f32r), sb("xt_lo", [P, KC, 2 * P], f32r)
        r_buf, l_buf, a_buf = two("r_buf", [P, 2 * P]), two("l_buf", [P, 2 * P]), two("a_buf", [P, 2 * P])
        a_hi, a_lo = ([sb(f"{n}{k}", [P, 2 * P], f32r) for k in range(NA)] for n in ("a_hi", "a_lo"))
        resid = sb("resid", [P, 2, DIM])
        y1, y2 = sb("y1", [P, 2, DIM]), sb("y2", [P, 2, DIM])

        sn = bank("sn")
        stp = [bank("st0"), bank("st1")]
        pv = bank("pv")
        misc = bank("misc")
        hps = [bank("h0"), bank("h1")]
        ops_ = bank("ops")
        sn_first = [sn, ops_, *hps]

        s_cst, s_len, s_wr = sem("cst_in"), sem("len_in"), sem("router_in")
        s_wraw = sems("w_raw_in")
        s_x, s_kv, s_v, s_keep = sems("x_in"), sems("kv_in"), sems("v_in"), sems("keep_in")
        s_qscr, s_kscr = sems("q_scr_written"), sems("k_scr_written")
        s_qst, s_kst = sems("q_stack_in"), sems("k_stack_in")
        s_out = sem("out_written")
        s_passed = sem("waits_passed")
        s_lenf, s_lenln, s_scale, s_wrd = sem("len_f"), sem("len_ln"), sem("scale_ready"), sem("router_diff")
        s_whi, s_wlo_v, s_wlo_p = sem("w_hi_done"), sem("w_lo_by_vector"), sem("w_lo_by_pool")
        s_zero, s_vzero, s_pick = sems("k_stack_zeroed"), sem("v_pad_zeroed"), sem("pick_rows")
        s_xst, s_xmv, s_xvar, s_xln, s_xrs, s_xn1, s_xn2, s_xsc = (
            sem(n) for n in ("x_stats", "x_moments", "x_var", "x_ln", "x_rstd0", "x_newton1", "x_newton2", "x_scale"))
        s_qf, s_qhi, s_qlo, s_khi, s_klo = (sem(n) for n in ("q_f", "q_hi", "q_lo", "k_hi", "k_lo"))
        s_vpad = sem("v_pad_ready")
        s_sn, s_max, s_nmhi, s_nmlo = sem("scores_qk"), sem("max_done"), sem("negmax_hi"), sem("negmax_lo")
        s_mt, s_mrows = sem("max_transposed"), sem("max_rows")
        s_st, s_exp = sem("scores_kq"), sem("exp_done")
        s_pv = sem("pv_done")
        s_dln, s_dinv, s_t1, s_t2, s_att, s_x2 = (
            sem(n) for n in ("den_ln", "den_inv0", "den_newton1", "den_inv", "attn_out", "x2_ready"))
        s_yst, s_ymv, s_yvar, s_yln, s_yrs, s_yn1, s_yn2, s_ysc = (
            sem(n) for n in ("y_stats", "y_moments", "y_var", "y_ln", "y_rstd0", "y_newton1", "y_newton2", "y_scale"))
        s_x2n, s_logit = sem("x2n_ready"), sem("logit_ready")
        s_nabs, s_ecoef, s_e1, s_wtop, s_c1, s_coef = (
            sem(n) for n in ("neg_abs", "coef_exp", "coef_sum", "top_weight", "coef_1", "coefs_ready"))
        s_xt, s_xthi, s_xtlo = sem("xt_transposed"), sem("xt_hi_ready"), sem("xt_lo_ready")
        s_h, s_r, s_l, s_a, s_ahi, s_alo = (
            sem(n) for n in ("h_ready", "relu_ready", "leaky_ready", "square_ready", "a_hi_ready", "a_lo_ready"))
        s_f2 = sem("a_buffers_free")
        s_o, s_ofree, s_resid, s_y1, s_y2 = (
            sem(n) for n in ("expert_out", "expert_out_free", "resid_ready", "y1_ready", "y2_ready"))

        def wait(eng, s, value):
            if not (isinstance(value, int) and value <= 0):
                eng.wait_ge(s, value)

        def wait_alone(eng, s, value):
            if not (isinstance(value, int) and value <= 0):
                eng.wait_ge(s, value)
                if not isinstance(value, int):
                    eng.sem_inc(s_passed, 1)

        def run_steps(eng, first_step, step):
            first_step()
            with eng.Fori(1, STEPS - 1) as i:
                step(i, last=False)
            step(STEPS - 1, last=True)

        block = stack.enter_context(nc.Block())

        @block.sync
        def _(sp):
            def batch(t, u, j):
                at = t[2 * u + j] if isinstance(u, int) else t[bass.ds(u * 2 + j, 1)].rearrange("o p n -> (o p) n")
                return at

            def load(u, j):
                m = u * 2 + j
                wait_alone(sp, s_qf, m - 1)
                sp.dma_start(x_raw[j][:, :], batch(x, u, j)).then_inc(s_x[j], 16)
                wait_alone(sp, s_khi, m - 1)
                wait_alone(sp, s_klo, m - 1)
                sp.dma_start(kv_raw[j][:, :], batch(ctx_kv, u, j)).then_inc(s_kv[j], 16)

            def load_v(u, j):
                wait_alone(sp, s_vpad, u * 2 + j - 1)
                sp.dma_start(v_raw[j][:, :, :], batch(ctx_t, u, j).rearrange("(c p) n -> p c n", p=P)).then_inc(s_v[j], 16)

            def stack_k(u, j):
                m = u * 2 + j
                wait_alone(sp, s_kst[j], 96 * u)
                wait_alone(sp, s_khi, m + 1)
                sp.dma_start(k_scr[j][0], k_hi[j][:, :].bitcast(f32)).then_inc(s_kscr[j], 16)
                wait_alone(sp, s_klo, m + 1)
                sp.dma_start(k_scr[j][1], k_lo[j][:, :].bitcast(f32)).then_inc(s_kscr[j], 16)

            def stack_q(u, j):
                m = u * 2 + j
                wait_alone(sp, s_qst[j], 48 * u)
                wait_alone(sp, s_qhi, m + 1)
                sp.dma_start(q_scr[j][0], q_hi[j][:, :].bitcast(f32)).then_inc(s_qscr[j], 16)
                wait_alone(sp, s_qlo, m + 1)
                sp.dma_start(q_scr[j][1], q_lo[j][:, :].bitcast(f32)).then_inc(s_qscr[j], 16)

            def read_k(u, j):
                wait_alone(sp, s_st, 8 * (u * 2 + j) - 8)
                wait_alone(sp, s_kscr[j], 32 * u + 32)
                for e in range(2):
                    for blk, part in enumerate((0, 1, 0)):
                        src = k_scr[j][part].rearrange("(g e r) n -> e r g n", g=PAIRS, e=2)[e]
                        row = 32 * blk + HD * e
                        sp.dma_start(k_st[j][row:row + HD, e, :, :].bitcast(f32), src).then_inc(s_kst[j], 16)

            def read_q(u, j):
                wait_alone(sp, s_st, 8 * (u * 2 + j) - 8)
                wait_alone(sp, s_qscr[j], 32 * u + 32)
                for blk, part in enumerate((0, 0, 1)):
                    src = q_scr[j][part].rearrange("(g r) n -> r g n", g=PAIRS)
                    sp.dma_start(q_st[j][32 * blk:32 * blk + 32, :, :].bitcast(f32), src).then_inc(s_qst[j], 16)

            def keep(u, j):
                wait_alone(sp, s_x2, u * 2 + j - 1)
                sp.dma_start(x_keep[j][:, :], batch(x, u, j)).then_inc(s_keep[j], 16)

            def store(g):
                wait_alone(sp, s_y2, g + 1)
                dst = (out[2 * g:2 * g + 2] if isinstance(g, int) else out[bass.ds(g * 2, 2)]).rearrange("t p n -> p t n")
                sp.dma_start(dst, y2[:, :, :]).then_inc(s_out, 16)

            load(0, 0)
            sp.dma_start(cst[:, :], consts).then_inc(s_cst, 16)
            load(0, 1)
            stack_k(0, 0)
            stack_q(0, 0)
            sp.wait_ge(s_zero[0], 1)
            read_k(0, 0)
            read_q(0, 0)
            stack_k(0, 1)
            stack_q(0, 1)
            sp.wait_ge(s_zero[1], 1)
            read_k(0, 1)
            read_q(0, 1)
            load_v(0, 0)
            load(1, 0)
            load_v(0, 1)
            load(1, 1)
            keep(0, 0)
            keep(0, 1)
            def weights(w):
                dst = w_raw[w][:, :].rearrange("p (c n) -> p c n", c=(KC, CHUNKS)[w])
                sp.dma_start(dst, (w_fc_t, w_proj_t)[w].rearrange("(c p) n -> p c n", p=P)).then_inc(s_wraw[w], 16)

            weights(0)

            def stacks(u, j):
                stack_k(u, j)
                stack_q(u, j)
                read_k(u, j)
                read_q(u, j)

            def first_step():
                for j in range(2):
                    stacks(1, j)
                    load_v(1, j)
                    if j == 0:
                        weights(1)

            def step(i, last):
                for j in range(2):
                    if not last:
                        load(i + 1, j)
                    keep(i, j)
                    if not last:
                        stacks(i + 1, j)
                        load_v(i + 1, j)
                store(i - 1)

            run_steps(sp, first_step, step)
            store(STEPS - 1)
            sp.wait_ge(s_out, 16 * STEPS)

        @block.gpsimd
        def _(pool):
            pool.memset(k_st[1][:, :, :, :].bitcast(f32), 0.0).then_inc(s_zero[1], 1)
            pool.memset(v_pad[0][:, :, :], 0.0).then_inc(s_vzero, 1)
            pool.memset(v_pad[1][:, :, :], 0.0).then_inc(s_vzero, 1)

            def split_k(u, j):
                m = u * 2 + j
                pool.wait_ge(s_khi, m + 1)
                wait(pool, s_kscr[j], 32 * u)
                pool.tensor_tensor(k_lo[j][:, :], kv_raw[j][:, :], k_hi[j][:, :].bitcast(f32), ALU.subtract).then_inc(s_klo, 1)

            def pad_v(u, j):
                m = u * 2 + j
                pool.wait_ge(s_v[j], 16 * u + 16)
                wait_alone(pool, s_pv, 2 * m - 2)
                src = v_raw[j][:, :, :].rearrange("p c (g n) -> p (c g) n", g=PAIRS)
                pool.tensor_copy(v_pad[j][:, :, 0:16], src[:, :, 0:16])
                pool.tensor_copy(v_pad[j][:, :, 48:64], src[:, :, 16:32]).then_inc(s_vpad, 1)

            def split_w(w, n):
                at = slice(n * WPIECE, (n + 1) * WPIECE)
                pool.wait_ge(s_whi, w * N_WPIECES + n + 1)
                pool.tensor_tensor(w_lo[w][:, at], w_raw[w][:, at], w_hi[w][:, at].bitcast(f32), ALU.subtract).then_inc(s_wlo_p, 1)

            def square(g, c):
                pool.wait_ge(s_l, g * 16 + (c + 1))
                pool.tensor_tensor(a_buf[c % 2][:, :], l_buf[c % 2][:, :], l_buf[c % 2][:, :], ALU.mult).then_inc(s_a, 1)

            split_k(0, 0)
            split_k(0, 1)
            pool.wait_ge(s_vzero, 2)
            pad_v(0, 0)
            pad_v(0, 1)

            def first_step():
                split_k(1, 0)
                split_w(0, 0)
                split_w(0, 1)
                split_w(0, 2)
                split_w(0, 3)
                pad_v(1, 0)

                split_k(1, 1)
                split_w(1, 0)
                split_w(1, 1)
                split_w(1, 2)
                split_w(1, 3)
                pad_v(1, 1)

            def step(i, last):
                for j in range(2):
                    square(i - 1, CH * j + 0)
                    square(i - 1, CH * j + 1)
                    if not last:
                        split_k(i + 1, j)
                    square(i - 1, CH * j + 2)
                    square(i - 1, CH * j + 3)
                    square(i - 1, CH * j + 4)
                    square(i - 1, CH * j + 5)
                    square(i - 1, CH * j + 6)
                    square(i - 1, CH * j + 7)
                    if not last:
                        pad_v(i + 1, j)

            run_steps(pool, first_step, step)
            for c in range(CHUNKS):
                square(STEPS - 1, c)

        @block.scalar
        def _(act):
            def k_part_hi(u, j):
                m = u * 2 + j
                act.wait_ge(s_kv[j], 16 * u + 16)
                wait(act, s_kscr[j], 32 * u)
                act.activation(k_hi[j][:, :], kv_raw[j][:, :], ACT.Copy).then_inc(s_khi, 1)

            def q_part_hi(u, j):
                m = u * 2 + j
                act.wait_ge(s_qf, m + 1)
                wait(act, s_qscr[j], 32 * u)
                act.activation(q_hi[j][:, :], q_f[j][:, :], ACT.Copy).then_inc(s_qhi, 1)

            def x_ln(u, j):
                act.wait_ge(s_xvar, u * 2 + j + 1)
                act.activation(xln[j][:, :], xvar[j][:, :], ACT.Ln).then_inc(s_xln, 1)

            def x_rstd(u, j):
                act.wait_ge(s_xln, u * 2 + j + 1)
                act.activation(xrs[j][:, :], xln[j][:, :], ACT.Exp, scale=-0.5).then_inc(s_xrs, 1)

            def y_ln(i, j):
                act.wait_ge(s_yvar, i * 2 + (j + 1))
                act.activation(yln[j][:, :], yvar[j][:, :], ACT.Ln).then_inc(s_yln, 1)

            def y_rstd(i, j):
                act.wait_ge(s_yln, i * 2 + (j + 1))
                act.activation(yrs[j][:, :], yln[j][:, :], ACT.Exp, scale=-0.5).then_inc(s_yrs, 1)

            def max_rows(i, j):
                b = i * 2 + j
                act.wait_ge(s_mt, b + 1)
                act.wait_ge(s_qst[j], 48 * i + 48)
                act.activation(q_st[j][MBLK:STACK, :, :],
                               misc[0:2 * HEADS, 0:DIM].unsqueeze(1).to_broadcast([2 * HEADS, PAIRS, DIM]),
                               ACT.Copy).then_inc(s_mrows, 1)

            def exp(i, j, k):
                b = i * 2 + j
                act.wait_ge(s_st, 8 * b + (k + 1))
                wait(act, s_pv, b * 2 - 1 if k < 4 else b * 2)
                act.activation(probs[HEAD_ORDER[k]][:, :, :], stp[k % 2][:, :].rearrange("p (c n) -> p c n", c=KC),
                               ACT.Exp).then_inc(s_exp, 1)

            def den_ln(i, j):
                b = i * 2 + j
                act.wait_ge(s_pv, b * 2 + 2)
                wait(act, s_t2, b)
                act.activation(dln[:, :], pv[:, DIM:2 * DIM], ACT.Ln).then_inc(s_dln, 1)

            def den_inverse(i, j):
                act.wait_ge(s_dln, i * 2 + (j + 1))
                act.activation(dinv[:, :], dln[:, :], ACT.Exp, scale=-1.0).then_inc(s_dinv, 1)

            def relu(g, c):
                act.wait_ge(s_h, g * 16 + (c + 1))
                act.activation(r_buf[c % 2][:, :], hps[c % 2][:, 0:2 * P], ACT.Relu, scale=0.5).then_inc(s_r, 1)

            def square_hi(g, c):
                act.wait_ge(s_l, g * 16 + (c + 1))
                act.wait_ge(s_f2, g * 16 + (c + 1))
                act.activation(a_hi[c % NA][:, :], l_buf[c % 2][:, :], ACT.Square).then_inc(s_ahi, 1)

            def coef_exp(g):
                act.wait_ge(s_nabs, g + 1)
                act.activation(ecoef[:, :], nabs[:, :], ACT.Exp).then_inc(s_ecoef, 1)

            def xt_part_hi(i):
                act.wait_ge(s_xt, i + 1)
                act.activation(xt_hi[:, :, :], misc[:, :].rearrange("p (c n) -> p c n", c=KC), ACT.Copy).then_inc(s_xthi, 1)

            def split_w(w, n):
                at = slice(n * WPIECE, (n + 1) * WPIECE)
                act.wait_ge(s_wraw[w], 16)
                act.activation(w_hi[w][:, at], w_raw[w][:, at], ACT.Copy).then_inc(s_whi, 1)

            def pick_rows(j):
                act.activation(k_st[j][MBLK:STACK, :, :, :].rearrange("p e g n -> p (e g) n"),
                               pick.unsqueeze(2).to_broadcast([2 * HEADS, HEADS, KEYS]), ACT.Copy).then_inc(s_pick, 1)

            act.preload_act_table_set("natural_log_exp_and_others")
            act.dma_start(len_i[:, :], k_len.partition_broadcast(P)).then_inc(s_len, 16)
            act.dma_start(wr[:, :, :], w_router.partition_broadcast(P)).then_inc(s_wr, 16)
            k_part_hi(0, 0)
            act.wait_ge(s_lenf, 1)
            act.activation(len_ln[:, :], len_f[:, :], ACT.Ln).then_inc(s_lenln, 1)
            x_ln(0, 0)
            x_rstd(0, 0)
            q_part_hi(0, 0)
            k_part_hi(0, 1)
            x_ln(0, 1)
            x_rstd(0, 1)
            q_part_hi(0, 1)
            act.wait_ge(s_cst, 16)
            for j in range(2):
                act.wait_ge(s_zero[j], 1)
                pick_rows(j)

            max_rows(0, 0)

            def first_step():
                exp(0, 0, 0)
                k_part_hi(1, 0)
                exp(0, 0, 1)
                exp(0, 0, 2)
                x_ln(1, 0)
                exp(0, 0, 3)
                exp(0, 0, 4)
                exp(0, 0, 5)
                exp(0, 0, 6)
                x_rstd(1, 0)
                exp(0, 0, 7)
                q_part_hi(1, 0)
                split_w(0, 0)
                split_w(0, 1)
                den_ln(0, 0)
                den_inverse(0, 0)
                max_rows(0, 1)
                split_w(0, 2)
                split_w(0, 3)
                y_ln(0, 0)
                y_rstd(0, 0)

                exp(0, 1, 0)
                exp(0, 1, 1)
                exp(0, 1, 2)
                exp(0, 1, 3)
                exp(0, 1, 4)
                exp(0, 1, 5)
                k_part_hi(1, 1)
                x_ln(1, 1)
                x_rstd(1, 1)
                exp(0, 1, 6)
                exp(0, 1, 7)
                split_w(1, 0)
                q_part_hi(1, 1)
                den_ln(0, 1)
                den_inverse(0, 1)
                split_w(1, 1)
                split_w(1, 2)
                y_ln(0, 1)
                y_rstd(0, 1)
                max_rows(1, 0)
                split_w(1, 3)
                xt_part_hi(0)

            def step(i, last):
                for j in range(2):
                    ahead = not (last and j == 1)
                    exp(i, j, 0)
                    exp(i, j, 1)
                    relu(i - 1, CH * j + 0)
                    relu(i - 1, CH * j + 1)
                    exp(i, j, 2)
                    exp(i, j, 3)
                    square_hi(i - 1, CH * j + 0)
                    square_hi(i - 1, CH * j + 1)
                    exp(i, j, 4)
                    relu(i - 1, CH * j + 2)
                    exp(i, j, 5)
                    if j == 0:
                        coef_exp(i - 1)
                    if not last:
                        k_part_hi(i + 1, j)
                        x_ln(i + 1, j)
                        x_rstd(i + 1, j)
                    exp(i, j, 6)
                    exp(i, j, 7)
                    relu(i - 1, CH * j + 3)
                    square_hi(i - 1, CH * j + 2)
                    if not last:
                        q_part_hi(i + 1, j)
                    square_hi(i - 1, CH * j + 3)
                    den_ln(i, j)
                    den_inverse(i, j)
                    relu(i - 1, CH * j + 4)
                    square_hi(i - 1, CH * j + 4)
                    relu(i - 1, CH * j + 5)
                    relu(i - 1, CH * j + 6)
                    y_ln(i, j)
                    y_rstd(i, j)
                    square_hi(i - 1, CH * j + 5)
                    if ahead:
                        max_rows(i + j, 1 - j)
                    relu(i - 1, CH * j + 7)
                    square_hi(i - 1, CH * j + 6)
                    square_hi(i - 1, CH * j + 7)
                xt_part_hi(i)

            run_steps(act, first_step, step)
            g = STEPS - 1
            for c in range(CHUNKS):
                relu(g, c)
                if c > 0:
                    square_hi(g, c - 1)
                if c == 0:
                    coef_exp(g)
            square_hi(g, CHUNKS - 1)

        @block.vector
        def _(dve):
            def moments(stage, m, src, st, mv, var, s_st_, s_mv_, s_var_):
                if stage == 0:
                    dve.bn_stats(st[:, :], src).then_inc(s_st_, 1)
                elif stage == 1:
                    wait_alone(dve, s_st_, m + 1)
                    dve.bn_aggr(mv[:, :], st[:, :]).then_inc(s_mv_, 1)
                else:
                    dve.wait_ge(s_mv_, m + 1)
                    dve.tensor_scalar(var[:, :], mv[:, 1:2], EPS, None, ALU.add).then_inc(s_var_, 1)

            def newton(stage, m, var, rs, n1, n2, sc, extra, s_rs_, s_n1_, s_n2_, s_sc_):
                if stage == 0:
                    dve.wait_ge(s_rs_, m + 1)
                    dve.scalar_tensor_tensor(n1[:, :], rs[:, :], rs[:, 0:1], var[:, :], ALU.mult, ALU.mult).then_inc(s_n1_, 1)
                elif stage == 1:
                    dve.wait_ge(s_n1_, m + 1)
                    dve.tensor_scalar(n2[:, :], n1[:, :], -0.5, 1.5, ALU.mult, ALU.add).then_inc(s_n2_, 1)
                else:
                    dve.wait_ge(s_n2_, m + 1)
                    dve.scalar_tensor_tensor(sc[:, :], n2[:, :], extra, rs[:, :], ALU.mult, ALU.mult).then_inc(s_sc_, 1)

            def x_moments(u, j, stage):
                if stage == 0:
                    dve.wait_ge(s_x[j], 16 * u + 16)
                moments(stage, u * 2 + j, x_raw[j][:, :], xst[j], xmv[j], xvar[j], s_xst, s_xmv, s_xvar)

            def x_newton(u, j, stage):
                m = u * 2 + j
                sc_b = scale_b[:, m:m + 1] if isinstance(u, int) else scale_b[:, bass.ds(m, 1)]
                newton(stage, m, xvar[j], xrs[j], xn1[j], xn2[j], xsc[j], sc_b, s_xrs, s_xn1, s_xn2, s_xsc)

            def q_normalise(u, j):
                dve.wait_ge(s_xsc, u * 2 + j + 1)
                dve.tensor_scalar(q_f[j][:, :], x_raw[j][:, :], xmv[j][:, 0:1], xsc[j][:, 0:1],
                                  ALU.subtract, ALU.mult).then_inc(s_qf, 1)

            def q_part_lo(u, j):
                m = u * 2 + j
                dve.wait_ge(s_qhi, m + 1)
                wait(dve, s_qscr[j], 32 * u)
                dve.tensor_tensor(q_lo[j][:, :], q_f[j][:, :], q_hi[j][:, :].bitcast(f32), ALU.subtract).then_inc(s_qlo, 1)

            def row_max(n, j, h, banks=[sn]):
                dve.wait_ge(s_sn, 8 * n + (h + 1))
                dve.tensor_reduce(negm[j][:, :, h], banks[h % len(banks)][:, :].rearrange("p (c n) -> p c n", c=KC),
                                  AX.X, ALU.max, negate=True).then_inc(s_max, 1)

            def split_max_hi(n, j):
                dve.wait_ge(s_max, 8 * n + 8)
                dve.tensor_copy(nm_r[j][:, :, 0, :], negm[j][:, :, :]).then_inc(s_nmhi, 1)

            def split_max_lo(n, j):
                dve.wait_ge(s_nmhi, n + 1)
                dve.tensor_tensor(nm_r[j][:, :, 1, :], negm[j][:, :, :], nm_r[j][:, :, 0, :].bitcast(f32),
                                  ALU.subtract).then_inc(s_nmlo, 1)

            def den_newton(i, j):
                dve.wait_ge(s_dinv, i * 2 + (j + 1))
                dve.tensor_tensor(t1[:, :], pv[:, DIM:2 * DIM], dinv[:, :], ALU.mult).then_inc(s_t1, 1)

            def den_inv(i, j):
                dve.wait_ge(s_t1, i * 2 + (j + 1))
                dve.scalar_tensor_tensor(t2[:, :], t1[:, :], -2.0, dinv[:, :], ALU.add, ALU.mult).then_inc(s_t2, 1)

            def attention_out(i, j):
                dve.wait_ge(s_t2, i * 2 + (j + 1))
                dve.tensor_tensor(att[:, :], pv[:, 0:DIM], t2[:, :], ALU.mult).then_inc(s_att, 1)

            def x2_sum(i, j):
                dve.wait_ge(s_att, i * 2 + (j + 1))
                dve.wait_ge(s_keep[j], 16 * i + 16)
                dve.tensor_tensor(x2[j][:, :], x_keep[j][:, :], att[:, :], ALU.subtract).then_inc(s_x2, 1)

            def x2_moments(i, j, stage):
                if stage == 0:
                    dve.wait_ge(s_x2, i * 2 + (j + 1))
                moments(stage, i * 2 + j, x2[j][:, :], yst[j], ymv[j], yvar[j], s_yst, s_ymv, s_yvar)

            def x2_newton(i, j, stage):
                newton(stage, i * 2 + j, yvar[j], yrs[j], yn1[j], yn2[j], ysc[j], 1.0, s_yrs, s_yn1, s_yn2, s_ysc)

            def x2_normalise(i, j):
                dve.wait_ge(s_ysc, i * 2 + (j + 1))
                dve.tensor_scalar(x2n[j][:, :], x2[j][:, :], ymv[j][:, 0:1], ysc[j][:, 0:1],
                                  ALU.subtract, ALU.mult).then_inc(s_x2n, 1)

            def router(i, j):
                dve.wait_ge(s_x2n, i * 2 + (j + 1))
                dve.scalar_tensor_tensor(dot_out[:, :], x2n[j][:, :], 1.0, wr_diff[:, :], ALU.mult, ALU.mult,
                                         accum_out=logit[:, j:j + 1]).then_inc(s_logit, 1)

            def neg_logit(g):
                dve.wait_ge(s_logit, g * 2 + 2)
                dve.tensor_scalar(e1[:, :], logit[:, :], -1.0, None, ALU.mult).then_inc(s_e1, 1)

            def neg_abs(g):
                dve.wait_ge(s_e1, g * 2 + 1)
                dve.tensor_tensor(nabs[:, :], logit[:, :], e1[:, :], ALU.min).then_inc(s_nabs, 1)

            def coef_sum(g):
                dve.wait_ge(s_ecoef, g + 1)
                dve.tensor_scalar(e1[:, :], ecoef[:, :], 1.0, None, ALU.add).then_inc(s_e1, 1)

            def top_weight(g):
                dve.wait_ge(s_e1, g * 2 + 2)
                dve.reciprocal(wtop[:, :], e1[:, :]).then_inc(s_wtop, 1)

            def coefs(g):
                dve.wait_ge(s_wtop, g + 1)
                dve.scalar_tensor_tensor(coef[1][:, :], logit[:, :], 0.0, wtop[:, :], ALU.is_gt, ALU.mult).then_inc(s_c1, 1)
                dve.scalar_tensor_tensor(coef[0][:, :], logit[:, :], 0.0, wtop[:, :], ALU.is_le, ALU.mult).then_inc(s_coef, 1)

            def residual_copy(g):
                dve.wait_ge(s_x2, g * 2 + 2)
                for t in range(2):
                    last = dve.tensor_copy(resid[:, t, :], x2[t][:, :])
                last.then_inc(s_resid, 1)

            def leaky(g, c):
                dve.wait_ge(s_r, g * 16 + (c + 1))
                dve.scalar_tensor_tensor(l_buf[c % 2][:, :], hps[c % 2][:, 0:2 * P], 0.5, r_buf[c % 2][:, :],
                                         ALU.mult, ALU.add).then_inc(s_l, 1)

            def square_lo(g, c):
                dve.wait_ge(s_a, g * 16 + (c + 1))
                dve.wait_ge(s_ahi, g * 16 + (c + 1))
                dve.tensor_tensor(a_lo[c % NA][:, :], a_buf[c % 2][:, :], a_hi[c % NA][:, :].bitcast(f32),
                                  ALU.subtract).then_inc(s_alo, 1)

            def expert_out(g, e):
                dve.wait_ge(s_o, g * 2 + (e + 1))
                if e == 0:
                    dve.wait_ge(s_coef, g + 1)
                    dve.wait_ge(s_resid, g + 1)
                    for t in range(2):
                        last = dve.scalar_tensor_tensor(y1[:, t, :], ops_[:, t * DIM:(t + 1) * DIM], coef[0][:, t:t + 1],
                                                        resid[:, t, :], ALU.mult, ALU.add)
                    last.then_inc(s_ofree, 1)
                else:
                    dve.wait_ge(s_c1, g + 1)
                    dve.wait_ge(s_ofree, g * 2 + 1)
                    wait(dve, s_out, 16 * g)
                    for t in range(2):
                        last = dve.scalar_tensor_tensor(y2[:, t, :], ops_[:, t * DIM:(t + 1) * DIM], coef[1][:, t:t + 1],
                                                        y1[:, t, :], ALU.mult, ALU.add)
                    last.then_inc(s_ofree, 1)
                    dve.wait_ge(s_ofree, g * 2 + 2)
                    dve.sem_inc(s_y2, 1)

            def xt_part_lo(i):
                dve.wait_ge(s_xthi, i + 1)
                dve.tensor_tensor(xt_lo[:, :, :], misc[:, :].rearrange("p (c n) -> p c n", c=KC),
                                  xt_hi[:, :, :].bitcast(f32), ALU.subtract).then_inc(s_xtlo, 1)

            dve.memset(k_st[0][:, :, :, :].bitcast(f32), 0.0).then_inc(s_zero[0], 1)
            for stage in range(3):
                x_moments(0, 0, stage)
            dve.wait_ge(s_len, 16)
            dve.tensor_copy(len_f[:, :], len_i[:, :]).then_inc(s_lenf, 1)
            dve.wait_ge(s_lenln, 1)
            dve.tensor_scalar(scale_b[:, :], len_ln[:, :], SCORE_SCALE, None, ALU.mult).then_inc(s_scale, 1)
            dve.wait_ge(s_scale, 1)
            for stage in range(3):
                x_newton(0, 0, stage)
            q_normalise(0, 0)
            for stage in range(3):
                x_moments(0, 1, stage)
            q_part_lo(0, 0)
            for stage in range(3):
                x_newton(0, 1, stage)
            q_normalise(0, 1)
            q_part_lo(0, 1)
            dve.wait_ge(s_wr, 16)
            dve.tensor_tensor(wr_diff[:, :], wr[:, 1, :], wr[:, 0, :], ALU.subtract).then_inc(s_wrd, 1)
            dve.wait_ge(s_wrd, 1)
            for h in range(HEADS):
                row_max(0, 0, h, sn_first)
            split_max_hi(0, 0)
            split_max_lo(0, 0)

            def first_step():
                x_moments(1, 0, 0)
                x_moments(1, 0, 1)
                x_moments(1, 0, 2)
                row_max(1, 1, 0, sn_first)
                row_max(1, 1, 1, sn_first)
                row_max(1, 1, 2, sn_first)
                row_max(1, 1, 3, sn_first)
                row_max(1, 1, 4, sn_first)
                x_newton(1, 0, 0)
                x_newton(1, 0, 1)
                x_newton(1, 0, 2)
                q_normalise(1, 0)
                row_max(1, 1, 5, sn_first)
                q_part_lo(1, 0)
                row_max(1, 1, 6, sn_first)
                row_max(1, 1, 7, sn_first)
                split_max_hi(1, 1)
                split_max_lo(1, 1)
                den_newton(0, 0)
                den_inv(0, 0)
                attention_out(0, 0)
                x2_sum(0, 0)
                x2_moments(0, 0, 0)
                x2_moments(0, 0, 1)
                x2_moments(0, 0, 2)
                x2_newton(0, 0, 0)
                x2_newton(0, 0, 1)
                x2_newton(0, 0, 2)
                x2_normalise(0, 0)
                router(0, 0)

                row_max(2, 0, 0, sn_first)
                row_max(2, 0, 1, sn_first)
                row_max(2, 0, 2, sn_first)
                row_max(2, 0, 3, sn_first)
                x_moments(1, 1, 0)
                x_moments(1, 1, 1)
                x_moments(1, 1, 2)
                row_max(2, 0, 4, sn_first)
                x_newton(1, 1, 0)
                x_newton(1, 1, 1)
                x_newton(1, 1, 2)
                q_normalise(1, 1)
                q_part_lo(1, 1)
                row_max(2, 0, 5, sn_first)
                row_max(2, 0, 6, sn_first)
                row_max(2, 0, 7, sn_first)
                den_newton(0, 1)
                den_inv(0, 1)
                split_max_hi(2, 0)
                attention_out(0, 1)
                x2_sum(0, 1)
                x2_moments(0, 1, 0)
                split_max_lo(2, 0)
                x2_moments(0, 1, 1)
                x2_moments(0, 1, 2)
                x2_newton(0, 1, 0)
                x2_newton(0, 1, 1)
                x2_newton(0, 1, 2)
                x2_normalise(0, 1)
                router(0, 1)
                xt_part_lo(0)

            def step(i, last):
                for j in range(2):
                    ahead = not (last and j == 1)
                    if ahead:
                        row_max(i * 2 + (j + 1), 1 - j, 0)
                    if j == 0:
                        residual_copy(i - 1)
                    if j == 1:
                        square_lo(i - 1, CH * j + -1)
                    leaky(i - 1, CH * j + 0)
                    if j == 0:
                        neg_logit(i - 1)
                    if ahead:
                        row_max(i * 2 + (j + 1), 1 - j, 1)
                    leaky(i - 1, CH * j + 1)
                    if j == 0:
                        neg_abs(i - 1)
                    if ahead:
                        row_max(i * 2 + (j + 1), 1 - j, 2)
                    square_lo(i - 1, CH * j + 0)
                    if not last:
                        x_moments(i + 1, j, 0)
                        x_moments(i + 1, j, 1)
                    square_lo(i - 1, CH * j + 1)
                    if not last:
                        x_moments(i + 1, j, 2)
                    if ahead:
                        row_max(i * 2 + (j + 1), 1 - j, 3)
                    if not last:
                        x_newton(i + 1, j, 0)
                        x_newton(i + 1, j, 1)
                    leaky(i - 1, CH * j + 2)
                    if j == 1:
                        expert_out(i - 1, 0)
                    if not last:
                        x_newton(i + 1, j, 2)
                        q_normalise(i + 1, j)
                    if ahead:
                        row_max(i * 2 + (j + 1), 1 - j, 4)
                    leaky(i - 1, CH * j + 3)
                    if not last:
                        q_part_lo(i + 1, j)
                    if ahead:
                        row_max(i * 2 + (j + 1), 1 - j, 5)
                    square_lo(i - 1, CH * j + 2)
                    square_lo(i - 1, CH * j + 3)
                    if ahead:
                        row_max(i * 2 + (j + 1), 1 - j, 6)
                    den_newton(i, j)
                    den_inv(i, j)
                    leaky(i - 1, CH * j + 4)
                    attention_out(i, j)
                    if j == 0:
                        coef_sum(i - 1)
                    x2_sum(i, j)
                    if ahead:
                        row_max(i * 2 + (j + 1), 1 - j, 7)
                    x2_moments(i, j, 0)
                    if ahead:
                        split_max_hi(i * 2 + (j + 1), 1 - j)
                    x2_moments(i, j, 1)
                    if ahead:
                        split_max_lo(i * 2 + (j + 1), 1 - j)
                    x2_moments(i, j, 2)
                    leaky(i - 1, CH * j + 5)
                    if j == 0:
                        top_weight(i - 1)
                    square_lo(i - 1, CH * j + 4)
                    x2_newton(i, j, 0)
                    x2_newton(i, j, 1)
                    x2_newton(i, j, 2)
                    leaky(i - 1, CH * j + 6)
                    if j == 0:
                        coefs(i - 1)
                    x2_normalise(i, j)
                    square_lo(i - 1, CH * j + 5)
                    leaky(i - 1, CH * j + 7)
                    square_lo(i - 1, CH * j + 6)
                    router(i, j)
                square_lo(i - 1, CHUNKS - 1)
                xt_part_lo(i)
                expert_out(i - 1, 1)

            run_steps(dve, first_step, step)
            g = STEPS - 1
            for c in range(CHUNKS):
                leaky(g, c)
                if c == 0:
                    neg_logit(g)
                    neg_abs(g)
                    residual_copy(g)
                if c == 1:
                    coef_sum(g)
                    top_weight(g)
                    coefs(g)
                if c > 0:
                    square_lo(g, c - 1)
                if c == CH + LAG - 1:
                    expert_out(g, 0)
            square_lo(g, CHUNKS - 1)
            expert_out(g, 1)

        @block.tensor
        def _(pe):
            def scores_qk(i, j, h, banks=[sn]):
                b = i * 2 + j
                if h == 0:
                    pe.wait_ge(s_qst[j], 48 * i + 48)
                    pe.wait_ge(s_kst[j], 96 * i + 96)
                wait(pe, s_max, 8 * b + (h - len(banks) + 1))
                for qc in range(KC):
                    last = pe.matmul(banks[h % len(banks)][:, qc * KEYS:(qc + 1) * KEYS],
                                     q_st[j][0:MBLK, h // 2, qc * P:(qc + 1) * P], k_st[j][0:MBLK, h % 2, h // 2, :],
                                     start=(qc == 0), stop=True, skip_group_check=True)
                last.then_inc(s_sn, 1)

            def max_transpose(i, j):
                b = i * 2 + j
                pe.wait_ge(s_nmlo, b + 1)
                wait(pe, s_mrows, b)
                wait(pe, s_xtlo, i - (1 - j))
                for qc in range(KC):
                    last = pe.transpose(misc[0:2 * HEADS, qc * P:(qc + 1) * P],
                                        nm_r[j][:, qc, :, :].rearrange("p a h -> p (a h)").bitcast(f32), ident)
                last.then_inc(s_mt, 1)

            def scores_kq(i, j, k):
                b, h = i * 2 + j, HEAD_ORDER[k]
                if k == 0:
                    pe.wait_ge(s_mrows, b + 1)
                wait(pe, s_exp, 8 * b + (k - 1))
                for kc in range(KC):
                    last = pe.matmul(stp[k % 2][:, kc * DIM:(kc + 1) * DIM],
                                     k_st[j][0:STACK, h % 2, h // 2, kc * P:(kc + 1) * P], q_st[j][0:STACK, h // 2, :],
                                     start=(kc == 0), stop=True, skip_group_check=True)
                last.then_inc(s_st, 1)

            def values(i, j, e, kc, den):
                b = i * 2 + j
                if kc == 0 and den == 0:
                    pe.wait_ge(s_exp, 8 * b + 4 + 4 * e)
                    if e == 0:
                        pe.wait_ge(s_vpad, b + 1)
                        wait(pe, s_att, b)
                for g in range(PAIRS):
                    lhs = ones_v[e] if den else v_pad[j][:, kc * PAIRS + g, 32 * e:32 * e + 32]
                    last = pe.matmul(pv[32 * g:32 * g + 32, den * DIM:(den + 1) * DIM], lhs, probs[2 * g + e][:, kc, :],
                                     start=(e == 0 and kc == 0 and den == 0), stop=(e == 1 and kc == 1),
                                     skip_group_check=True)
                if kc == 1 and den == 1:
                    last.then_inc(s_pv, 1)

            def ffn1(g, c):
                if c >= 2:
                    pe.wait_ge(s_l, g * 16 + (c - 1))
                if c == 0:
                    pe.wait_ge(s_xthi, g + 1)
                    pe.wait_ge(s_xtlo, g + 1)
                for kc in range(KC):
                    for w, xt in ((0, xt_hi), (1, xt_hi), (0, xt_lo)):
                        last = pe.matmul(hps[c % 2][:, 0:2 * P], wfc[w][:, kc, c * P:(c + 1) * P], xt[:, kc, :],
                                         start=(kc == 0 and w == 0 and xt is xt_hi), stop=(kc == KC - 1 and xt is xt_lo))
                last.then_inc(s_h, 1)

            def ffn2(g, c):
                pe.wait_ge(s_ahi, g * 16 + (c + 1))
                if c == 0:
                    pe.wait_ge(s_wlo_p, 2 * N_WPIECES)
                if c % CH == 0:
                    wait(pe, s_ofree, g * 2 + c // CH)
                for part in range(3):
                    if part == 2:
                        pe.wait_ge(s_alo, g * 16 + (c + 1))
                    for t in range(2):
                        a, w = ((a_hi, 0), (a_hi, 1), (a_lo, 0))[part]
                        last = pe.matmul(ops_[:, t * DIM:(t + 1) * DIM], a[c % NA][:, t * P:(t + 1) * P], wproj[w][:, c, :],
                                         start=(c % CH == 0 and part == 0 and t == 0), stop=(c % CH == CH - 1 and part == 2),
                                         skip_group_check=True)
                last.then_inc(s_f2, 1)
                if c % CH == CH - 1:
                    pe.wait_ge(s_f2, g * 16 + (c + 1 + NA))
                    pe.sem_inc(s_o, 1)

            def x_transpose(i, last):
                pe.wait_ge(s_x2n, i * 2 + 2)
                pe.wait_ge(s_mrows, i * 2 + (2 if last else 3))
                for t in range(2):
                    for kc in range(KC):
                        last = pe.transpose(misc[:, kc * 2 * P + t * P:kc * 2 * P + (t + 1) * P],
                                            x2n[t][:, kc * P:(kc + 1) * P], ident)
                last.then_inc(s_xt, 1)

            pe.sem_inc(s_f2, NA)
            pe.wait_ge(s_cst, 16)
            for h in range(HEADS):
                scores_qk(0, 0, h, sn_first)
            max_transpose(0, 0)
            pe.wait_ge(s_pick, 2)

            def first_step():
                scores_qk(0, 1, 0, sn_first)
                scores_kq(0, 0, 0)
                scores_qk(0, 1, 1, sn_first)
                scores_kq(0, 0, 1)
                scores_kq(0, 0, 2)
                scores_qk(0, 1, 2, sn_first)
                scores_kq(0, 0, 3)
                scores_kq(0, 0, 4)
                scores_qk(0, 1, 3, sn_first)
                scores_kq(0, 0, 5)
                scores_kq(0, 0, 6)
                values(0, 0, 0, 0, 0)
                scores_qk(0, 1, 4, sn_first)
                values(0, 0, 0, 0, 1)
                values(0, 0, 0, 1, 0)
                scores_kq(0, 0, 7)
                scores_qk(0, 1, 5, sn_first)
                scores_qk(0, 1, 6, sn_first)
                values(0, 0, 0, 1, 1)
                values(0, 0, 1, 0, 0)
                scores_qk(0, 1, 7, sn_first)
                values(0, 0, 1, 0, 1)
                values(0, 0, 1, 1, 0)
                values(0, 0, 1, 1, 1)
                max_transpose(0, 1)

                scores_kq(0, 1, 0)
                scores_kq(0, 1, 1)
                scores_qk(1, 0, 0, sn_first)
                scores_qk(1, 0, 1, sn_first)
                scores_qk(1, 0, 2, sn_first)
                scores_kq(0, 1, 2)
                scores_qk(1, 0, 3, sn_first)
                scores_kq(0, 1, 3)
                scores_kq(0, 1, 4)
                scores_qk(1, 0, 4, sn_first)
                scores_kq(0, 1, 5)
                values(0, 1, 0, 0, 0)
                scores_kq(0, 1, 6)
                scores_kq(0, 1, 7)
                values(0, 1, 0, 0, 1)
                scores_qk(1, 0, 5, sn_first)
                scores_qk(1, 0, 6, sn_first)
                values(0, 1, 0, 1, 0)
                values(0, 1, 0, 1, 1)
                values(0, 1, 1, 0, 0)
                values(0, 1, 1, 0, 1)
                values(0, 1, 1, 1, 0)
                values(0, 1, 1, 1, 1)
                scores_qk(1, 0, 7, sn_first)
                max_transpose(1, 0)
                x_transpose(0, False)
                pe.wait_ge(s_wlo_p, N_WPIECES)

            def step(i, last):
                for j in range(2):
                    ahead = not (last and j == 1)
                    scores_kq(i, j, 0)
                    if ahead:
                        scores_qk(i + j, 1 - j, 0)
                    scores_kq(i, j, 1)
                    ffn1(i - 1, CH * j + 0)
                    ffn1(i - 1, CH * j + 1)
                    if j == 1:
                        ffn2(i - 1, CH * j + 0 - LAG)
                    scores_kq(i, j, 2)
                    if ahead:
                        scores_qk(i + j, 1 - j, 1)
                    scores_kq(i, j, 3)
                    if j == 1:
                        ffn2(i - 1, CH * j + 1 - LAG)
                    ffn1(i - 1, CH * j + 2)
                    scores_kq(i, j, 4)
                    if ahead:
                        scores_qk(i + j, 1 - j, 2)
                    scores_kq(i, j, 5)
                    values(i, j, 0, 0, 0)
                    values(i, j, 0, 0, 1)
                    scores_kq(i, j, 6)
                    if ahead:
                        scores_qk(i + j, 1 - j, 3)
                    values(i, j, 0, 1, 0)
                    if j == 1:
                        ffn2(i - 1, CH * j + 2 - LAG)
                    scores_kq(i, j, 7)
                    ffn1(i - 1, CH * j + 3)
                    if ahead:
                        scores_qk(i + j, 1 - j, 4)
                    values(i, j, 0, 1, 1)
                    values(i, j, 1, 0, 0)
                    values(i, j, 1, 0, 1)
                    if ahead:
                        scores_qk(i + j, 1 - j, 5)
                    values(i, j, 1, 1, 0)
                    values(i, j, 1, 1, 1)
                    if ahead:
                        scores_qk(i + j, 1 - j, 6)
                    ffn1(i - 1, CH * j + 4)
                    ffn2(i - 1, CH * j + 3 - LAG)
                    if ahead:
                        scores_qk(i + j, 1 - j, 7)
                    ffn1(i - 1, CH * j + 5)
                    ffn2(i - 1, CH * j + 4 - LAG)
                    ffn1(i - 1, CH * j + 6)
                    ffn2(i - 1, CH * j + 5 - LAG)
                    ffn2(i - 1, CH * j + 6 - LAG)
                    if ahead:
                        max_transpose(i + j, 1 - j)
                    ffn1(i - 1, CH * j + 7)
                    ffn2(i - 1, CH * j + 7 - LAG)
                x_transpose(i, last)
                for c in range(CHUNKS - LAG, CHUNKS):
                    ffn2(i - 1, c)

            run_steps(pe, first_step, step)
            g = STEPS - 1
            for c in range(CHUNKS + LAG):
                if c < CHUNKS:
                    ffn1(g, c)
                if c >= LAG:
                    ffn2(g, c - LAG)


def kernel(**inputs):
    import numpy as np
    import concourse.bacc as bacc
    from concourse.bass_utils import run_bass_kernel_spmd

    ctx = inputs["ctx_2048"]
    consts = np.zeros((P, 200), np.float32)
    consts[:, 0:128] = np.eye(128, dtype=np.float32)
    for e in range(2):
        consts[:, 128 + 32 * e + HD * e:128 + 32 * e + HD * e + HD] = 1.0
    for part in range(2):
        for h in range(HEADS):
            consts[MBLK + HEADS * part + h, 192 + PAIRS * (h % 2) + h // 2] = 1.0
    arrays = {
        "x": np.ascontiguousarray(inputs["x"]),
        "ctx_kv": np.ascontiguousarray(ctx),
        "ctx_t": np.ascontiguousarray(np.transpose(ctx, (0, 2, 1))),
        "k_len": np.ascontiguousarray(inputs["itok_B_779_1933"]),
        "w_router": np.ascontiguousarray(inputs["L0_ffn_w_router"]),
        "w_fc_t": np.ascontiguousarray(np.transpose(inputs["L0_ffn_w_fc"], (2, 0, 1)).reshape(DIM, EXPERTS * HID)),
        "w_proj_t": np.ascontiguousarray(np.transpose(inputs["L0_ffn_w_proj"], (0, 2, 1)).reshape(EXPERTS * HID, DIM)),
        "consts": consts,
    }
    nc = bacc.Bacc("TRN2", target_bir_lowering=False, num_devices=1)
    aps = {n: nc.dram_tensor(n, a.shape, mybir.dt.from_np(a.dtype), kind="ExternalInput").ap() for n, a in arrays.items()}
    out = nc.dram_tensor("out", (B, ROWS, DIM), mybir.dt.float32, kind="ExternalOutput").ap()
    build(nc, aps["x"], aps["ctx_kv"], aps["ctx_t"], aps["k_len"], aps["w_router"], aps["w_fc_t"], aps["w_proj_t"],
          aps["consts"], out)
    r = run_bass_kernel_spmd(nc, [arrays], core_ids=[0])
    return r.results[0]["out"]
```
